# Optimizing a Trainium2 kernel written in Bass

```python
import numpy as np
import jax
import jax.numpy as jnp

def _softmax(x, axis=-1):
    return jax.nn.softmax(x, axis=axis)

def _gelu(x):
    return jax.nn.gelu(x, approximate=True)

def _silu(x):
    return jax.nn.silu(x)

def _sigmoid(x):
    return jax.nn.sigmoid(x)

def _layernorm(x, axis=-1, eps=1e-05):
    m = jnp.mean(x, axis=axis, keepdims=True)
    v = jnp.var(x, axis=axis, keepdims=True)
    return (x - m) / jnp.sqrt(v + eps)

def _scatter_add(tgt, idx, src, axis=0):
    return tgt.at[idx].add(src)

def _segment_sum(src, seg, n):
    return jax.ops.segment_sum(src, seg, n)
kernel_name = 'mk_perceiver_d1_seqx_r8_c4ef7a'

def setup_inputs(seed: int=0):
    np.random.seed(seed)
    _w = jnp.asarray

    def _rec_inputs():
        import jax
        import jax.numpy as jnp
        _rk = jax.random.key(seed)
        x = -0.0002928 + 1 * jax.random.normal(jax.random.fold_in(_rk, 1), (32, 64, 128), jnp.float32)
        _lenS = 64 - jax.random.randint(jax.random.fold_in(_rk, 7), (32,), 0, max(1, 64 // 4) + 1, jnp.int32)
        _lenS2 = 128 - jax.random.randint(jax.random.fold_in(_rk, 8), (32,), 0, max(1, 128 // 4) + 1, jnp.int32)
        _ctx_1024P = jax.random.normal(jax.random.fold_in(_rk, 11), (32, 16, 128), jnp.float32)
        _ctx_1024c = jax.random.dirichlet(jax.random.fold_in(_rk, 511), 0.3 * jnp.ones((16,), jnp.float32), (32, 128))
        _ctx_1024t = jnp.einsum('bsk,bkd->bsd', _ctx_1024c, _ctx_1024P)
        _ctx_1024t = _ctx_1024t * jax.lax.rsqrt(jnp.mean(jnp.square(_ctx_1024t)) + 1e-12) * 0.953939
        ctx_1024 = -1.39393e-06 + 0.999914 * (_ctx_1024t + 0.3 * jax.random.normal(jax.random.fold_in(_rk, 611), (32, 128, 128), jnp.float32))
        _validS = jnp.arange(64)[None, :] < _lenS[:, None]
        _validS2 = jnp.arange(128)[None, :] < _lenS2[:, None]
        _causal = jnp.tril(jnp.ones((64, 64), dtype=bool))
        mask_SxS2_ik0 = jnp.where(jnp.broadcast_to(_validS2[0:1, :], (64, 128)), 0, 1).astype(jnp.int32)
        return (x, ctx_1024, mask_SxS2_ik0)
    x, ctx_1024, mask_SxS2_ik0 = _rec_inputs()

    def _L0_xattn_setup():
        import jax, jax.numpy as jnp
        import numpy as np
        B, S, D, H = (2, 256, 128, 16)
        HD = D // H
        DENSITY = 0.1
        key = jax.random.key(seed)
        ks = jax.random.split(key, 12)
        scale = 0.02
        inp = {'query': jax.random.normal(ks[0], (B, S, D), jnp.float32), 'key': jax.random.normal(ks[1], (B, S, D), jnp.float32), 'value': jax.random.normal(ks[2], (B, S, D), jnp.float32)}
        m = jax.random.uniform(ks[3], (S, S)) < DENSITY
        m = m.at[jnp.arange(S), jnp.arange(S)].set(True)
        inp['mask'] = m.astype(jnp.int32)
        inp['Wq'] = jax.random.normal(ks[4], (D, D), jnp.float32) * scale
        inp['bq'] = jax.random.normal(ks[5], (D,), jnp.float32) * scale
        inp['Wk'] = jax.random.normal(ks[6], (D, D), jnp.float32) * scale
        inp['bk'] = jax.random.normal(ks[7], (D,), jnp.float32) * scale
        inp['Wv'] = jax.random.normal(ks[8], (D, D), jnp.float32) * scale
        inp['bv'] = jax.random.normal(ks[9], (D,), jnp.float32) * scale
        inp['Wo'] = jax.random.normal(ks[10], (D, D), jnp.float32) * scale
        inp['bo'] = jax.random.normal(ks[11], (D,), jnp.float32) * scale
        return inp
    _L0_xattn_all = _L0_xattn_setup()
    _L0_xattn_in = {k: v for k, v in _L0_xattn_all.items() if k in ('Wq', 'bq', 'Wk', 'bk', 'Wv', 'bv', 'Wo', 'bo')}
    del _L0_xattn_all

    def _L0_attn_setup():
        import jax, jax.numpy as jnp
        import numpy as np
        D_MODEL = 128
        D_HIDDEN = 32
        key = jax.random.key(seed)
        ks = jax.random.split(key, 10)
        B, T = (4, 512)
        s = lambda fan_in: 1.0 / np.sqrt(fan_in)
        return {'x': jax.random.normal(ks[0], (B, T, D_MODEL), dtype=jnp.float32), 'A': jnp.log(jnp.arange(1, D_HIDDEN + 1, dtype=jnp.float32)), 'Wb': jax.random.uniform(ks[1], (D_MODEL, D_HIDDEN), jnp.float32, -s(D_MODEL), s(D_MODEL)), 'bb': jax.random.uniform(ks[2], (D_HIDDEN,), jnp.float32, -s(D_MODEL), s(D_MODEL)), 'Wc': jax.random.uniform(ks[3], (D_HIDDEN, D_MODEL), jnp.float32, -s(D_HIDDEN), s(D_HIDDEN)), 'bc': jax.random.uniform(ks[4], (D_MODEL,), jnp.float32, -s(D_HIDDEN), s(D_HIDDEN)), 'Wd': jax.random.uniform(ks[5], (D_MODEL, D_MODEL), jnp.float32, -s(D_MODEL), s(D_MODEL)), 'bd': jax.random.uniform(ks[6], (D_MODEL,), jnp.float32, -s(D_MODEL), s(D_MODEL)), 'Wdelta': jax.random.uniform(ks[7], (D_MODEL, D_HIDDEN), jnp.float32, -s(D_MODEL), s(D_MODEL)), 'bdelta': jax.random.uniform(ks[8], (D_HIDDEN,), jnp.float32, -s(D_MODEL), s(D_MODEL))}
    _L0_attn_all = _L0_attn_setup()
    _L0_attn_in = {k: v for k, v in _L0_attn_all.items() if k in ('A', 'Wb', 'bb', 'Wc', 'bc', 'Wd', 'bd', 'Wdelta', 'bdelta')}
    del _L0_attn_all

    def _L0_ffn_setup():
        import jax, jax.numpy as jnp
        import numpy as np
        B, S, D, FF, E, L = (8, 256, 128, 512, 16, 4)

        def _unipool_layer(xt, router, W1, W2):
            logits = xt @ router
            probs = jax.nn.softmax(logits, axis=-1)
            w = jnp.max(probs, axis=-1)
            idx = jnp.argmax(probs, axis=-1)

            def body(acc, params):
                w1, w2, i = params
                h = jax.nn.silu(xt @ w1) @ w2
                sel = jnp.where(idx == i, w, 0.0)
                return (acc + sel[:, None] * h, None)
            out, _ = jax.lax.scan(body, jnp.zeros_like(xt), (W1, W2, jnp.arange(W1.shape[0])))
            return out
        key = jax.random.key(seed)
        k0, k1, k2, k3 = jax.random.split(key, 4)
        x = jax.random.normal(k0, (B, S, D), dtype=jnp.float32)
        routers = jax.random.normal(k1, (L, D, E), dtype=jnp.float32) * 0.02
        W1 = jax.random.normal(k2, (E, D, FF), dtype=jnp.float32) * 0.02
        W2 = jax.random.normal(k3, (E, FF, D), dtype=jnp.float32) * 0.02
        return {'x': x, 'routers': routers, 'W1': W1, 'W2': W2}
    _L0_ffn_all = _L0_ffn_setup()
    _L0_ffn_in = {k: v for k, v in _L0_ffn_all.items() if k in ('routers', 'W1', 'W2')}
    del _L0_ffn_all
    return {'x': x, 'ctx_1024': ctx_1024, 'mask_SxS2_ik0': mask_SxS2_ik0, 'L0_xattn_Wq': _L0_xattn_in['Wq'], 'L0_xattn_bq': _L0_xattn_in['bq'], 'L0_xattn_Wk': _L0_xattn_in['Wk'], 'L0_xattn_bk': _L0_xattn_in['bk'], 'L0_xattn_Wv': _L0_xattn_in['Wv'], 'L0_xattn_bv': _L0_xattn_in['bv'], 'L0_xattn_Wo': _L0_xattn_in['Wo'], 'L0_xattn_bo': _L0_xattn_in['bo'], 'L0_attn_A': _L0_attn_in['A'], 'L0_attn_Wb': _L0_attn_in['Wb'], 'L0_attn_bb': _L0_attn_in['bb'], 'L0_attn_Wc': _L0_attn_in['Wc'], 'L0_attn_bc': _L0_attn_in['bc'], 'L0_attn_Wd': _L0_attn_in['Wd'], 'L0_attn_bd': _L0_attn_in['bd'], 'L0_attn_Wdelta': _L0_attn_in['Wdelta'], 'L0_attn_bdelta': _L0_attn_in['bdelta'], 'L0_ffn_routers': _L0_ffn_in['routers'], 'L0_ffn_W1': _L0_ffn_in['W1'], 'L0_ffn_W2': _L0_ffn_in['W2']}

def reference(x, ctx_1024, mask_SxS2_ik0, L0_xattn_Wq, L0_xattn_bq, L0_xattn_Wk, L0_xattn_bk, L0_xattn_Wv, L0_xattn_bv, L0_xattn_Wo, L0_xattn_bo, L0_attn_A, L0_attn_Wb, L0_attn_bb, L0_attn_Wc, L0_attn_bc, L0_attn_Wd, L0_attn_bd, L0_attn_Wdelta, L0_attn_bdelta, L0_ffn_routers, L0_ffn_W1, L0_ffn_W2):
    import jax
    import jax.numpy as jnp

    def _L0_xattn_ref(query, key, value, mask, Wq, bq, Wk, bk, Wv, bv, Wo, bo):
        import jax, jax.numpy as jnp
        import numpy as np
        B, S, D, H = (2, 256, 128, 16)
        HD = D // H
        DENSITY = 0.1
        b = query.shape[0]
        q = (query @ Wq + bq).reshape(b, -1, H, HD).transpose(0, 2, 1, 3)
        k = (key @ Wk + bk).reshape(b, -1, H, HD).transpose(0, 2, 1, 3)
        v = (value @ Wv + bv).reshape(b, -1, H, HD).transpose(0, 2, 1, 3)
        keep = mask.astype(bool)
        scores = jnp.einsum('bhsd,bhtd->bhst', q, k) / jnp.sqrt(jnp.asarray(HD, q.dtype))
        neg = jnp.finfo(scores.dtype).min
        scores = jnp.where(keep[None, None], scores, neg)
        w = jax.nn.softmax(scores, axis=-1)
        w = jnp.where(keep[None, None], w, jnp.asarray(0, w.dtype))
        out = jnp.einsum('bhst,bhtd->bhsd', w, v)
        out = out.transpose(0, 2, 1, 3).reshape(b, -1, D)
        return out @ Wo + bo

    def _L0_attn_ref(x, A, Wb, bb, Wc, bc, Wd, bd, Wdelta, bdelta):
        import jax, jax.numpy as jnp
        import numpy as np
        D_MODEL = 128
        D_HIDDEN = 32
        delta = jax.nn.softplus(jnp.einsum('btc,ch->bth', x, Wdelta) + bdelta)
        A_log = -jax.nn.softplus(A)
        A_bar_log = delta * A_log
        B_bar = delta * (jnp.einsum('btc,ch->bth', x, Wb) + bb)
        A_log_cum = jnp.clip(jnp.cumsum(A_bar_log, axis=1), -20.0, 20.0)
        A_log_cum_shifted = jnp.concatenate([jnp.zeros_like(A_log_cum[:, :1, :]), A_log_cum[:, :-1, :]], axis=1)
        B_shift = B_bar * jnp.exp(-A_log_cum_shifted)
        h = jnp.exp(A_log_cum) * jnp.cumsum(B_shift, axis=1)
        out = jnp.einsum('bth,hc->btc', h, Wc) + bc + jnp.einsum('btc,cd->btd', x, Wd) + bd
        return out

    def _L0_ffn_ref(x, routers, W1, W2):
        import jax, jax.numpy as jnp
        import numpy as np
        B, S, D, FF, E, L = (8, 256, 128, 512, 16, 4)

        def _unipool_layer(xt, router, W1, W2):
            logits = xt @ router
            probs = jax.nn.softmax(logits, axis=-1)
            w = jnp.max(probs, axis=-1)
            idx = jnp.argmax(probs, axis=-1)

            def body(acc, params):
                w1, w2, i = params
                h = jax.nn.silu(xt @ w1) @ w2
                sel = jnp.where(idx == i, w, 0.0)
                return (acc + sel[:, None] * h, None)
            out, _ = jax.lax.scan(body, jnp.zeros_like(xt), (W1, W2, jnp.arange(W1.shape[0])))
            return out
        b, s, d = x.shape
        xt = x.reshape(-1, d)

        def step(carry, router):
            return (_unipool_layer(carry, router, W1, W2), None)
        xt, _ = jax.lax.scan(step, xt, routers)
        return xt.reshape(b, s, d)
    x = x + _L0_xattn_ref(_layernorm(x, axis=-1), ctx_1024, ctx_1024, mask_SxS2_ik0, L0_xattn_Wq, L0_xattn_bq, L0_xattn_Wk, L0_xattn_bk, L0_xattn_Wv, L0_xattn_bv, L0_xattn_Wo, L0_xattn_bo)
    x = x + _L0_attn_ref(_layernorm(x, axis=-1), L0_attn_A, L0_attn_Wb, L0_attn_bb, L0_attn_Wc, L0_attn_bc, L0_attn_Wd, L0_attn_bd, L0_attn_Wdelta, L0_attn_bdelta)
    x = x + _L0_ffn_ref(_layernorm(x, axis=-1), L0_ffn_routers, L0_ffn_W1, L0_ffn_W2)
    return x

_drawn_inputs = setup_inputs


def setup_inputs(seed=0):
    import zlib

    import numpy as np

    out = dict(_drawn_inputs(seed))
    spreads = {}
    factors = {}
    for name, (base, spread) in spreads.items():
        noise = np.random.default_rng([zlib.crc32(name.encode()), seed]).standard_normal(out[name].shape)
        drawn = base * np.exp(spread * noise) if base else spread * noise
        out[name] = jnp.asarray(drawn.astype(out[name].dtype))
    for name, factor in factors.items():
        out[name] = (out[name] * factor).astype(out[name].dtype)
    return out
```

```python
from contextlib import ExitStack

import concourse.bass as bass
from concourse import mybir

P = 128
F32 = mybir.dt.float32
BF16 = mybir.dt.bfloat16
I32 = mybir.dt.int32
ACT = mybir.ActivationFunctionType
ALU = mybir.AluOpType
AX = mybir.AxisListType.X

EPS = 1e-5
MASKED = -1e30
HEADS = 16


def ds(start, size):
    return bass.ds(start, size)


def perceiver_block(nc, x, ctx, mask, Wq, bq, Wk, bk, Wv, bv, Wo, bo, A, Wb, bb, Wc, bc, Wd, bd,
                    Wdelta, bdelta, routers, W1, W2, out):
    B, S, D = x.shape
    T = ctx.shape[1]
    HD = D // HEADS
    H = A.shape[0]
    L, _, E = routers.shape
    FF = W1.shape[2]
    N = B * S
    NT = N // P
    BT = P // S
    NG = P // H
    GT = NT // NG
    GW = GT * P
    SLOTS = NT + E - 1
    SP2 = 32
    FC = FF // P
    PAIRS = HEADS // 2
    NV = 5
    DUMP = N
    ROWS = N + SP2 * P
    assert D == P and T == P and S * 2 == P and NG == 4 and E == 16 and L % 2 == 0

    x_t = x.rearrange("b s d -> (b s) d").rearrange("(t p) d -> p t d", p=P)
    out_t = out.rearrange("b s d -> (b s) d").rearrange("(t p) d -> p t d", p=P)
    ctx_t = ctx.rearrange("b t d -> t b d")
    rows = [nc.dram_tensor(f"token_rows_{i}", (ROWS, D), F32, kind="Internal").ap() for i in range(2)]

    def col(v):
        return v.rearrange("(n a) -> n a", a=1)

    with ExitStack() as stack:
        def sb(name, shape, dt=F32):
            return stack.enter_context(nc.sbuf_tensor(name, shape, dt))

        def sem(name):
            return stack.enter_context(nc.semaphore(name))

        banks = [stack.enter_context(nc.psum_tensor(f"bank{i}", [P, 512], F32)) for i in range(8)]

        wq, wk, wv, wo, wd = (sb(n, [P, D]) for n in ("wq", "wk", "wv", "wo", "wd"))
        wdl, wb = sb("wdl", [D, H]), sb("wb", [D, H])
        wc4 = sb("wc4", [P, D])
        w1 = sb("w1", [P, E * FF])
        w2 = sb("w2", [P, E * FF])
        rt = sb("rt", [P, L, E])
        rnow = sb("rnow", [P, 32])
        bqc, bkc = sb("bqc", [P, 1]), sb("bkc", [P, 1])
        bvr, bor, bcr, bdr = (sb(n, [P, D]) for n in ("bvr", "bor", "bcr", "bdr"))
        bdl4, bb4, a4 = sb("bdl4", [P, 1]), sb("bb4", [P, 1]), sb("a4", [P, 1])
        a_tmp = sb("a_tmp", [P, 4])
        ident = sb("ident", [P, P])
        ones = sb("ones", [P, P])
        onesb = sb("onesb", [P, P], BF16)
        trib = sb("trib", [P, P], BF16)
        pair_rows = sb("pair_rows", [P, P], BF16)
        mask_i = sb("mask_i", [S, T], I32)
        mask_bias = sb("mask_bias", [P, T], BF16)
        keep = sb("keep", [S, T])
        keep_any = sb("keep_any", [S, P])
        head_of = sb("head_of", [P, HEADS])
        local = sb("local", [P, 4])
        diag = sb("diag", [P, 2, 4, S])
        iota_r = sb("iota_r", [P, P])
        iota_e = sb("iota_e", [P, E])
        rev_e = sb("rev_e", [P, E])
        thr_gt = sb("thr_gt", [P, 16])
        thr_ge = sb("thr_ge", [P, 16])
        iota_j = sb("iota_j", [P, SP2])
        dump_row = sb("dump_row", [P, SP2])
        not_first = sb("not_first", [P, GW])
        not_first16 = sb("not_first16", [P, 256])
        vals = sb("vals", [P, NT, NV])
        xs = sb("xs", [P, NT, D])
        cur = sb("cur", [P, NT, D])
        curT = sb("curT", [P, N])
        st = sb("st", [P, NT, 6])
        mean = sb("mean", [P, NT])
        half_gap = sb("half_gap", [P, NT])
        rstd = sb("rstd", [P, NT])
        xln = sb("xln", [P, 2, D])
        cx = sb("cx", [P, 2, BT, D])
        aT = sb("aT", [P, 2, 3 * P])
        qT = sb("qT", [P, 2, P])
        qm = sb("qm", [P, 2, BT * HEADS * S])
        kT = sb("kT", [P, 2, BT * T])
        vv = sb("vv", [P, 2, BT * D])
        nmax = sb("nmax", [P, 2, 4])
        pp = sb("pp", [P, 2, 512])
        ppT = sb("ppT", [P, 4, 512])
        od = sb("od", [P, 512])
        od_s = sb("od_s", [P, 2, 2, BT, S])
        rden = sb("rden", [P, BT * S])
        attnT = sb("attnT", [P, 2, P])
        sA, sB, sC, sD = (sb(n, [P, GW]) for n in ("sA", "sB", "sC", "sD"))
        decay = sb("decay", [P, GW // S, S + 1])
        lgT = sb("lgT", [P, 512])
        lg, ex, pr, eq, tot, inc, exc, cmp, rk = (sb(n, [P, 256]) for n in
                                                  ("lg", "ex", "pr", "eq", "tot", "inc", "exc", "cmp", "rk"))
        ohb = sb("ohb", [P, 256], BF16)
        mx, sm, wt, fm, nt, itl, tb, rank, jb, jo, jj, rr, wr = (sb(n, [P, 16]) for n in
            ("mx", "sm", "wt", "fm", "nt", "itl", "tb", "rank", "jb", "jo", "jj", "rr", "wr"))
        wpart = sb("wpart", [P, 3, 16], BF16)
        ohr = sb("ohr", [P, NT, P], BF16)
        ohj = sb("ohj", [P, NT, SP2])
        carried = sb("carried", [P, NT, NV, SP2], BF16)
        inv = sb("inv", [P, NV, SP2])
        pad = sb("pad", [P, SP2])
        tok = sb("tok", [P, SP2])
        wslot = sb("wslot", [P, SP2])
        gidx = sb("gidx", [P, SP2], I32)
        sidx = sb("sidx", [P, SP2], I32)
        scmp = sb("scmp", [1, SP2, E])
        sef = sb("sef", [1, SP2])
        slot_expert = sb("slot_expert", [1, SP2], I32)
        gcol = sb("gcol", [P, 4], I32)
        scol = sb("scol", [P, 4], I32)
        xin = sb("xin", [P, 4, D])
        yout = sb("yout", [P, 4, D])
        xT = sb("xT", [P, 2, P])
        th = sb("th", [P, 2, FF])
        hh = sb("hh", [P, 2, FF])
        hT = sb("hT", [P, 2, FF])

        names = """x_loaded w_loaded w1_loaded w2_loaded stored rows_stored
            consts_pool consts_dve consts_mm dve_step act_step
            stats_ready rstd_ready ln_ready
            xln_ready tr_done a_evac proj_done q_evac k_evac v_evac qm_ready s_done sub_done exp_done
            pt_done pt_evac od_done od_read attn_ready wo_done x_updated
            t_done t_evac scan_mm scan_abs scan_soft scan_cum scan_exp scan_h scan_out x2_ready
            cur_loaded router_ready logits_done lgT_ready lg_done sh_ready ex_ready oh_ready rank_mm
            inv_in inv_done tables_ready expert_ready
            nmax_ready od_summed rden_ready xo_ready
            waited_alone gcol_ready scol_ready xT_mm xT_evac h_mm tanh_done h_ready hT_mm hT_evac y_mm y_ready
            out_ready""".split()
        s = dict(zip(names, [sem(n) for n in names]))
        ctx_loaded = [sem(f"ctx_loaded{u}") for u in range(2)]
        gathered = [sem(f"gathered{u}") for u in range(4)]
        scattered = [sem(f"scattered{u}") for u in range(4)]
        per_u = [len(range(u, SLOTS, 4)) for u in range(4)]

        small = [(wq[:], Wq), (wk[:], Wk), (wv[:], Wv), (wo[:], Wo), (wd[:], Wd),
                 (wdl[:], Wdelta), (wb[:], Wb), (rt[:], routers.rearrange("l d e -> d l e")),
                 (bqc[:], col(bq)), (bkc[:], col(bk)), (mask_i[:], mask),
                 (bvr[:], bv.partition_broadcast(P)), (bor[:], bo.partition_broadcast(P)),
                 (bcr[:], bc.partition_broadcast(P)), (bdr[:], bd.partition_broadcast(P))]
        small += [(dst[g * H:(g + 1) * H, :], src) for g in range(NG)
                  for dst, src in ((wc4, Wc), (bdl4, col(bdelta)), (bb4, col(bb)), (a4, col(A)))]
        W_SMALL = 16 * len(small)

        def pairs_of_tiles(eng, body, first, last):
            body(0, 0, first=True, last=False)
            body(1, 1, first=False, last=False)
            with eng.Fori(2, NT - 3, 2) as t:
                body(t, 0, first=False, last=False)
                body(t + 1, 1, first=False, last=False)
            body(NT - 2, 0, first=False, last=False)
            body(NT - 1, 1, first=False, last=True)

        def layers(eng, body):
            with eng.Fori(0, L // 2) as two:
                for parity in range(2):
                    body(two * 2 + parity, parity, two)

        def slot_steps(eng, step, depth, lo, loops):
            for i in range(lo):
                step(i, i % 4)
            with eng.Fori(lo, lo + 4 * loops - 3, 4) as i:
                for k in range(4):
                    step(i + k, (lo + k) % 4)
            for i in range(lo + 4 * loops, SLOTS + depth):
                step(i, i % 4)

        def has(i, lag, lo, loops):
            return not isinstance(i, int) or 0 <= i - lag < SLOTS

        def wait_alone(eng, which, value):
            eng.wait_ge(which, value)
            eng.sem_inc(s["waited_alone"], 1)

        block = stack.enter_context(nc.Block())

        @block.sync
        def _(sp):
            sp.dma_start(xs[:], x_t).then_inc(s["x_loaded"], 16)
            for dst, src in small:
                sp.dma_start(dst, src).then_inc(s["w_loaded"], 16)

            def load_ctx(t, u, first, last):
                if not isinstance(t, int) or t >= 2:
                    wait_alone(sp, s["tr_done"], t - 1)
                sp.dma_start(cx[:, u, :, :], ctx_t[:, ds(t * BT, BT), :]).then_inc(ctx_loaded[u], 16)

            load_ctx(0, 0, True, False)
            load_ctx(1, 1, True, False)
            sp.dma_start(w1[:].rearrange("p (e f) -> p e f", e=E), W1.rearrange("e d f -> d e f")) \
                .then_inc(s["w1_loaded"], 16)
            sp.dma_start(w2[:].rearrange("p (e c d) -> p e c d", e=E, c=FC),
                         W2.rearrange("e (c p) d -> p e c d", p=P)).then_inc(s["w2_loaded"], 16)
            with sp.Fori(2, NT - 1, 2) as t:
                load_ctx(t, 0, False, False)
                load_ctx(t + 1, 1, False, False)
            sp.wait_ge(s["ln_ready"], 2 * NT)
            sp.dma_start(rows[0][0:N, :].rearrange("(t p) d -> p t d", p=P), cur[:]) \
                .then_inc(s["rows_stored"], 16)
            sp.wait_ge(s["rows_stored"], 16)

            def load_rows(parity, layer):
                if parity == 1:
                    for u in range(4):
                        wait_alone(sp, scattered[u], layer * (16 * per_u[u]))
                    wait_alone(sp, s["t_done"], (layer + 1) * 4)
                sp.dma_start(cur[:], rows[parity][0:N, :].rearrange("(t p) d -> p t d", p=P)) \
                    .then_inc(s["cur_loaded"], 16)

            def two_layers(two):
                load_rows(0, two * 2)
                load_rows(1, two * 2 + 1)
                for u in range(4):
                    wait_alone(sp, scattered[u], (two + 1) * (32 * per_u[u]))

            with sp.Fori(0, L // 2) as two:
                two_layers(two)
            sp.dma_start(cur[:], rows[0][0:N, :].rearrange("(t p) d -> p t d", p=P)) \
                .then_inc(s["cur_loaded"], 16)
            for half in range(2):
                sp.wait_ge(s["out_ready"], half + 1)
                a = slice(half * NT // 2, (half + 1) * NT // 2)
                sp.dma_start(out_t[:, a, :], xs[:, a, :]).then_inc(s["stored"], 16)
            sp.wait_ge(s["stored"], 32)

        @block.gpsimd
        def _(pool):
            g = nc.gpsimd
            g.memset(ident[:], 0.0)
            g.memset(ones[:], 1.0)
            g.memset(onesb[:], 1.0)
            g.memset(head_of[:], 1.0)
            g.memset(mask_bias[:], 0.0)
            g.memset(rnow[:], 0.0)
            g.memset(not_first[:], 1.0)
            g.memset(not_first16[:], 1.0)
            g.memset(decay[:], 1.0).then_inc(s["consts_pool"], 1)
            for dst, pat, base, cm in [
                    (iota_r[:], [[1, P]], 0, 0), (iota_e[:], [[1, E]], 0, 0), (rev_e[:], [[-1, E]], E, 0),
                    (thr_gt[:], [[P, 16]], 0, 0), (thr_ge[:], [[P, 16]], P, 0), (iota_j[:], [[1, SP2]], 0, 0),
                    (dump_row[:], [[P, SP2]], DUMP + 1, 1),
                    (vals[:, :, 0], [[0, NT]], 1, 1), (vals[:, :, 1], [[1, NT]], 0, 0)]:
                last = g.iota(dst, pattern=pat, base=base, channel_multiplier=cm,
                              allow_small_or_imprecise_dtypes=True)
            last.then_inc(s["consts_pool"], 1)
            pool.wait_ge(s["consts_pool"], 2)
            g.affine_select(out=ident[:], in_=ident[:], compare_op=ALU.not_equal, fill=1.0, base=0,
                            pattern=[[-1, P]], channel_multiplier=1)
            g.affine_select(out=trib[:], in_=onesb[:], compare_op=ALU.is_gt, fill=0.0, base=0,
                            pattern=[[1, P]], channel_multiplier=-1)
            g.affine_select(out=head_of[:], in_=head_of[:], compare_op=ALU.is_ge, fill=0.0, base=0,
                            pattern=[[-HD, HEADS]], channel_multiplier=1).then_inc(s["consts_pool"], 1)
            pool.wait_ge(s["consts_pool"], 3)
            g.affine_select(out=head_of[:], in_=head_of[:], compare_op=ALU.is_ge, fill=0.0, base=HD - 1,
                            pattern=[[HD, HEADS]], channel_multiplier=-1)
            nf = not_first[:].rearrange("p (b t) -> p b t", t=S)
            g.memset(nf[:, :, 0:1], 0.0)
            nf16 = not_first16[:].rearrange("p (e k) -> p e k", k=NT)
            g.memset(nf16[:, :, 0:1], 0.0)
            g.tensor_copy(pair_rows[:, 0:S], ident[:, 0:S])
            g.tensor_copy(pair_rows[:, S:P], ident[:, 0:S]).then_inc(s["consts_pool"], 1)

            def masked_queries(t, u, first, last):
                pool.wait_ge(s["q_evac"], t + 1)
                if not isinstance(t, int) or t >= 2:
                    pool.wait_ge(s["s_done"], 4 * (t - 1))
                for b in range(BT):
                    w = HEADS * S
                    last_op = g.tensor_tensor(
                        qm[:, u, b * w:(b + 1) * w].rearrange("p (h s) -> p h s", h=HEADS),
                        qT[:, u, b * S:(b + 1) * S].unsqueeze(1).broadcast_to([P, HEADS, S]),
                        head_of[:].unsqueeze(2).broadcast_to([P, HEADS, S]), ALU.mult)
                last_op.then_inc(s["qm_ready"], 1)

            pairs_of_tiles(pool, masked_queries, None, None)

            LO, LOOPS, LAG = 6, 6, 6

            def one_layer(layer, parity, two):
                src, dst = rows[parity], rows[1 - parity]

                def step(i, u):
                    if has(i, 0, LO, LOOPS):
                        if not isinstance(i, int) or i >= 4:
                            wait_alone(pool, s["xT_mm"], layer * SLOTS + (i - 3))
                        elif i == 0:
                            wait_alone(pool, s["tables_ready"], layer + 1)
                        g.tensor_copy(gcol[:, u:u + 1], gidx[:, ds(i, 1)]).then_inc(s["gcol_ready"], 1)
                        wait_alone(pool, s["gcol_ready"], layer * SLOTS + (i + 1))
                        g.indirect_dma_start(
                            out=xin[:, u, :], out_offset=None, in_=src[0:N, :],
                            in_offset=bass.IndirectOffsetOnAxis(ap=gcol[:, u:u + 1], axis=0)) \
                            .then_inc(gathered[u], 16)
                    if has(i, LAG, LO, LOOPS):
                        j, v = i - LAG, (u - LAG) % 4
                        wait_alone(pool, s["y_ready"], layer * SLOTS + (j + 1))
                        g.tensor_copy(scol[:, v:v + 1], sidx[:, ds(j, 1)]).then_inc(s["scol_ready"], 1)
                        wait_alone(pool, s["scol_ready"], layer * SLOTS + (j + 1))
                        g.indirect_dma_start(
                            out=dst, out_offset=bass.IndirectOffsetOnAxis(ap=scol[:, v:v + 1], axis=0),
                            in_=yout[:, v, :], in_offset=None).then_inc(scattered[v], 16)

                slot_steps(pool, step, LAG, LO, LOOPS)

            layers(pool, one_layer)

        def scatter_count(layer, j, v):
            return layer * (16 * per_u[v]) + (j - v) * 4 + 16

        @block.scalar
        def _(act):
            a = nc.scalar
            act.wait_ge(s["w_loaded"], W_SMALL)
            act.wait_ge(s["consts_pool"], 4)
            def rstd_of(n):
                act.wait_ge(s["stats_ready"], n)
                a.activation(rstd[:], rstd[:], ACT.Ln).then_inc(s["act_step"], 1)
                step[0] += 1
                act.wait_ge(s["act_step"], step[0])
                a.activation(rstd[:], rstd[:], ACT.Exp, scale=-0.5).then_inc(s["rstd_ready"], 1)

            step = [0]
            rstd_of(1)
            a.mul(bqc[:], bqc[:], float(HD) ** -0.5).then_inc(s["act_step"], 1)
            step[0] += 1
            act.wait_ge(s["act_step"], step[0])

            def evac_inputs(t, u):
                act.wait_ge(s["tr_done"], t + 1)
                if not isinstance(t, int) or t >= 2:
                    act.wait_ge(s["proj_done"], t - 1)
                a.copy(aT[:, u, :], banks[5][:, 0:3 * P]).then_inc(s["a_evac"], 1)

            def evac_qk(t, u):
                act.wait_ge(s["proj_done"], t + 1)
                if not isinstance(t, int) or t >= 2:
                    act.wait_ge(s["qm_ready"], t - 1)
                    act.wait_ge(s["s_done"], 4 * (t - 1))
                a.activation(qT[:, u, :], banks[6][:, 0:P], ACT.Identity, bias=bqc[:, 0:1],
                             scale=float(HD) ** -0.5).then_inc(s["q_evac"], 1)
                a.activation(kT[:, u, :], banks[6][:, P:3 * P], ACT.Identity, bias=bkc[:, 0:1],
                             scale=1.0).then_inc(s["k_evac"], 1)

            def exp_scores(n, u2):
                act.wait_ge(s["sub_done"], n + 1)
                a.activation(pp[:, u2, :], pp[:, u2, :], ACT.Exp).then_inc(s["exp_done"], 1)

            def evac_pt(n, u4, read):
                act.wait_ge(s["pt_done"], n + 1)
                if read is not None:
                    act.wait_ge(s["od_done"], read)
                a.copy(ppT[:, u4, :], banks[2 + u4 % 2][:, :]).then_inc(s["pt_evac"], 1)

            def tile(t, u, first, last):
                n = 4 * t
                for i in range(4):
                    if not (first and i < 2):
                        evac_pt(n + (i - 2), (i - 2) % 4,
                                None if isinstance(t, int) and n + i < 6 else 2 * t + ((i - 2) // 2 - 1))
                    exp_scores(n + i, i % 2)
                    if i == 1 and not last:
                        evac_inputs(t + 1, 1 - u)
                    if i == 2 and not last:
                        evac_qk(t + 1, 1 - u)

            evac_inputs(0, 0)
            evac_qk(0, 0)
            pairs_of_tiles(act, tile, None, None)
            evac_pt(4 * NT - 2, 2, 2 * NT - 2)
            evac_pt(4 * NT - 1, 3, 2 * NT - 2)

            def evac_tiles(done, first_dve):
                for q in (0, 2):
                    act.wait_ge(s["t_done"], done + q + 1)
                    a.copy(curT[:, q * 512:(q + 1) * 512], banks[q][:, :]).then_inc(s["t_evac"], 1)

            rstd_of(2)
            evac_tiles(0, None)
            a.activation(a_tmp[:, 0:1], a4[:], ACT.Abs)
            act.wait_ge(s["scan_mm"], 1)
            a.activation(sC[:], banks[4][:, :], ACT.Abs, bias=bdl4[:, 0:1]).then_inc(s["scan_abs"], 1)
            act.wait_ge(s["scan_abs"], 1)
            a.activation(sC[:], sC[:], ACT.Exp, scale=-1.0).then_inc(s["act_step"], 1)
            step[0] += 1
            act.wait_ge(s["act_step"], step[0])
            a.activation(sC[:], sC[:], ACT.Ln, bias=1.0).then_inc(s["act_step"], 1)
            step[0] += 1
            a.activation(a_tmp[:, 1:2], a_tmp[:, 0:1], ACT.Exp, scale=-1.0).then_inc(s["act_step"], 1)
            step[0] += 1
            act.wait_ge(s["act_step"], step[0])
            a.activation(a_tmp[:, 2:3], a_tmp[:, 1:2], ACT.Ln, bias=1.0).then_inc(s["scan_soft"], 1)
            act.wait_ge(s["scan_cum"], 1)
            a.activation(decay[:, :, 1:S + 1], sD[:].rearrange("p (b t) -> p b t", t=S), ACT.Exp,
                         scale=-1.0).then_inc(s["scan_exp"], 1)
            a.activation(sA[:], sD[:], ACT.Exp).then_inc(s["scan_exp"], 1)
            rstd_of(3)

            def one_layer(layer, parity, two):
                done = layer * 4 + 4
                for q in (0, 2):
                    act.wait_ge(s["t_done"], done + (q + 1))
                    a.copy(curT[:, q * 512:(q + 1) * 512], banks[q][:, :]).then_inc(s["t_evac"], 1)
                act.wait_ge(s["sh_ready"], layer + 1)
                a.activation(ex[:], ex[:], ACT.Exp).then_inc(s["ex_ready"], 1)

                def step(i, u):
                    if has(i, 0, 7, 6):
                        act.wait_ge(s["xT_mm"], layer * SLOTS + (i + 1))
                        if not isinstance(i, int) or i >= 2:
                            act.wait_ge(s["h_mm"], layer * SLOTS + (i - 1))
                        a.copy(xT[:, u % 2, :], banks[u % 2][:, 0:P]).then_inc(s["xT_evac"], 1)
                    if has(i, 1, 7, 6):
                        j, v = i - 1, (u - 1) % 2
                        act.wait_ge(s["h_mm"], layer * SLOTS + (j + 1))
                        if not isinstance(i, int) or j >= 2:
                            act.wait_ge(s["h_ready"], layer * SLOTS + (j - 1))
                        a.activation(th[:, v, :], banks[2 + v][:, :], ACT.Tanh, scale=0.5) \
                            .then_inc(s["tanh_done"], 1)

                slot_steps(act, step, 3, 7, 6)

            layers(act, one_layer)

        @block.tensor
        def _(pe):
            mm = nc.tensor.matmul
            pe.wait_ge(s["w_loaded"], W_SMALL)
            pe.wait_ge(s["consts_pool"], 4)
            pe.wait_ge(s["consts_dve"], 1)
            mm(banks[7][:, 0:S], keep_any[:, :], ident[0:S, 0:S], start=True, stop=True) \
                .then_inc(s["consts_mm"], 1)

            def transposes_in(t, u):
                pe.wait_ge(s["xln_ready"], t + 1)
                pe.wait_ge(ctx_loaded[u], (t - u) * 8 + 16)
                if not isinstance(t, int) or t >= 1:
                    pe.wait_ge(s["a_evac"], t)
                if not isinstance(t, int) or t >= 3:
                    pe.wait_ge(s["x_updated"], t - 2)
                nc.tensor.transpose(banks[5][:, 0:P], xln[:, u, :], ident[:])
                nc.tensor.transpose(banks[5][:, P:2 * P], cx[:, u, 0, :], ident[:])
                nc.tensor.transpose(banks[5][:, 2 * P:3 * P], cx[:, u, 1, :], ident[:]) \
                    .then_inc(s["tr_done"], 1)

            def project(t, u):
                pe.wait_ge(s["a_evac"], t + 1)
                if not isinstance(t, int) or t >= 1:
                    pe.wait_ge(s["k_evac"], t)
                    pe.wait_ge(s["v_evac"], t)
                else:
                    pe.wait_ge(s["consts_dve"], 2)
                for b in range(BT):
                    mm(banks[7][:, b * D:(b + 1) * D], aT[:, u, (1 + b) * P:(2 + b) * P], wv[:],
                       start=True, stop=True)
                mm(banks[6][:, 0:P], wq[:], aT[:, u, 0:P], start=True, stop=True)
                mm(banks[6][:, P:3 * P], wk[:], aT[:, u, P:3 * P], start=True, stop=True) \
                    .then_inc(s["proj_done"], 1)

            def scores(t, u, i, first):
                n = 4 * t + i
                b, half = i // 2, i % 2
                if i == 0:
                    pe.wait_ge(s["qm_ready"], t + 1)
                    pe.wait_ge(s["k_evac"], t + 1)
                if not (first and i < 2):
                    pe.wait_ge(s["sub_done"], n - 1)
                bank = banks[i % 2]
                mm(bank[:, :].rearrange("p (k t) -> p k t", k=4), pair_rows[:],
                   mask_bias[:].unsqueeze(1).broadcast_to([P, 4, T]), start=True, stop=False)
                for k in range(4):
                    c = ((b * HEADS) + (half * 4 + k) * 2) * S
                    last = mm(bank[:, k * T:(k + 1) * T], qm[:, u, c:c + P], kT[:, u, b * T:(b + 1) * T],
                              start=False, stop=(k == 3))
                last.then_inc(s["s_done"], 1)

            def transpose_probs(n, i4, early):
                pe.wait_ge(s["exp_done"], n + 1)
                if not early:
                    pe.wait_ge(s["pt_evac"], n - 1)
                for k in range(4):
                    last = nc.tensor.transpose(banks[2 + i4 % 2][:, k * P:(k + 1) * P],
                                               pp[:, i4 % 2, k * P:(k + 1) * P], ident[:])
                last.then_inc(s["pt_done"], 1)

            def values(t, u, b, early):
                pe.wait_ge(s["pt_evac"], 4 * t + 2 * b + 2)
                if b == 0:
                    pe.wait_ge(s["v_evac"], t + 1)
                if not early:
                    pe.wait_ge(s["od_read"], 2 * t + b)
                for which in range(2):
                    for g in range(4):
                        lhsT = vv[:, u, b * D + 32 * g:b * D + 32 * g + 32] if which == 0 else ones[:, 0:32]
                        src = ppT[:, 2 * b + g // 2, (g % 2) * 256:(g % 2) * 256 + 256]
                        last = mm(banks[4][32 * g:32 * g + 32, which * 256:(which + 1) * 256], lhsT, src,
                                  start=True, stop=True)
                last.then_inc(s["od_done"], 1)

            def project_out(t, u):
                pe.wait_ge(s["attn_ready"], t + 1)
                mm(banks[5][:, 0:D], attnT[:, u, :], wo[:], start=True, stop=True).then_inc(s["wo_done"], 1)

            def tile(t, u, first, last):
                n = 4 * t
                scores(t, u, 0, first)
                if not first:
                    transpose_probs(n - 2, 2, False)
                scores(t, u, 1, first)
                if not first:
                    transpose_probs(n - 1, 3, False)
                    values(t - 1, 1 - u, 1, False)
                if not last:
                    transposes_in(t + 1, 1 - u)
                scores(t, u, 2, False)
                transpose_probs(n, 0, first)
                if not last:
                    project(t + 1, 1 - u)
                if not first:
                    if last:
                        pe.wait_ge(s["a_evac"], NT)
                    project_out(t - 1, 1 - u)
                scores(t, u, 3, False)
                transpose_probs(n + 1, 1, first)
                values(t, u, 0, first)

            transposes_in(0, 0)
            project(0, 0)
            pairs_of_tiles(pe, tile, None, None)
            transpose_probs(4 * NT - 2, 2, False)
            transpose_probs(4 * NT - 1, 3, False)
            values(NT - 1, 1, 1, False)
            pe.wait_ge(s["x_updated"], NT - 1)
            project_out(NT - 1, 1)

            def transpose_tiles():
                for q in range(4):
                    for k in range(4):
                        last = nc.tensor.transpose(banks[q][:, k * P:(k + 1) * P], cur[:, 4 * q + k, :],
                                                   ident[:])
                    last.then_inc(s["t_done"], 1)

            pe.wait_ge(s["ln_ready"], NT)
            transpose_tiles()
            pe.wait_ge(s["t_evac"], 4)
            for w, bank in ((wdl, banks[4]), (wb, banks[5])):
                for g in range(NG):
                    last = mm(bank[H * g:H * (g + 1), :], w[:], curT[:, g * GW:(g + 1) * GW],
                              start=True, stop=True)
                last.then_inc(s["scan_mm"], 1)
            pe.wait_ge(s["scan_h"], 1)
            for k in range(NT):
                g, c = k // GT, k % GT
                bank = banks[k // 4]
                part = bank[:, (k % 4) * P:(k % 4 + 1) * P]
                mm(part, sC[H * g:H * (g + 1), c * P:(c + 1) * P], wc4[H * g:H * (g + 1), :],
                   start=True, stop=False)
                last = mm(part, curT[:, k * P:(k + 1) * P], wd[:], start=False, stop=True)
                if k % 4 == 3:
                    last.then_inc(s["scan_out"], 1)

            pe.wait_ge(s["w1_loaded"], 16)
            pe.wait_ge(s["w2_loaded"], 16)
            pe.wait_ge(s["x2_ready"], 4)

            def one_layer(layer, parity, two):
                pe.wait_ge(s["cur_loaded"], (layer + 1) * 16)
                transpose_tiles()
                pe.wait_ge(s["t_evac"], layer * 4 + 8)
                pe.wait_ge(s["router_ready"], layer + 1)
                for g in range(4):
                    last = mm(banks[4][32 * g:32 * g + 32, :], rnow[:], curT[:, g * 512:(g + 1) * 512],
                              start=True, stop=True)
                last.then_inc(s["logits_done"], 1)
                pe.wait_ge(s["lgT_ready"], layer + 1)
                for c in range(4):
                    last = nc.tensor.transpose(banks[5][:, c * P:(c + 1) * P], lgT[:, c * P:(c + 1) * P],
                                               ident[:])
                last.then_inc(s["lg_done"], 1)
                pe.wait_ge(s["oh_ready"], layer + 1)
                mm(banks[6][:, 0:256], trib[:], ohb[:], start=True, stop=True)
                mm(banks[7][:, 0:256], onesb[:], ohb[:], start=True, stop=True).then_inc(s["rank_mm"], 1)
                pe.wait_ge(s["inv_in"], layer + 1)
                for k in range(NT):
                    last = mm(banks[4][:, 0:NV * SP2], ohr[:, k, :],
                              carried[:, k, :, :].rearrange("p v j -> p (v j)"),
                              start=(k == 0), stop=(k == NT - 1))
                last.then_inc(s["inv_done"], 1)
                pe.wait_ge(s["expert_ready"], layer + 1)

                def expert_of(j):
                    return nc.values_load(
                        slot_expert[0:1, ds(j, 1)], engines=[mybir.EngineType.PE], min_val=0, max_val=E - 1,
                        skip_runtime_bounds_check_because="the vector engine bounds it by E - 1")

                def count(j):
                    return layer * SLOTS + j

                def step(i, u):
                    inner = not isinstance(i, int)
                    if has(i, 0, 7, 6):
                        pe.wait_ge(gathered[u], scatter_count(layer, i, u))
                        if inner or i >= 2:
                            pe.wait_ge(s["xT_evac"], count(i - 1))
                        nc.tensor.transpose(banks[u % 2][:, 0:P], xin[:, u, :], ident[:]) \
                            .then_inc(s["xT_mm"], 1)
                    if has(i, 1, 7, 6):
                        j, v = i - 1, (u - 1) % 2
                        e = expert_of(j)
                        pe.wait_ge(s["xT_evac"], count(j + 1))
                        if inner or j >= 2:
                            pe.wait_ge(s["h_ready"], count(j - 1))
                        mm(banks[2 + v][:, :], xT[:, v, :], w1[:, ds(e * FF, FF)], start=True, stop=True) \
                            .then_inc(s["h_mm"], 1)
                    if has(i, 2, 7, 6):
                        j, v = i - 2, u % 2
                        pe.wait_ge(s["h_ready"], count(j + 1))
                        if inner or j >= 2:
                            pe.wait_ge(s["hT_evac"], count(j - 1))
                        for c in range(FC):
                            last = nc.tensor.transpose(banks[4 + v][:, c * P:(c + 1) * P],
                                                       hh[:, v, c * P:(c + 1) * P], ident[:])
                        last.then_inc(s["hT_mm"], 1)
                    if has(i, 3, 7, 6):
                        j, v = i - 3, (u - 3) % 2
                        e = expert_of(j)
                        pe.wait_ge(s["hT_evac"], count(j + 1))
                        if inner or j >= 2:
                            pe.wait_ge(s["y_ready"], count(j - 1))
                        for c in range(FC):
                            last = mm(banks[6 + v][:, 0:D], hT[:, v, c * P:(c + 1) * P],
                                      w2[:, ds(e * FF + c * P, P)], start=(c == 0), stop=(c == FC - 1))
                        last.then_inc(s["y_mm"], 1)

                slot_steps(pe, step, 3, 7, 6)

            layers(pe, one_layer)

        @block.vector
        def _(dve):
            v = nc.vector
            step = [0]

            def link(ins):
                ins.then_inc(s["dve_step"], 1)
                step[0] += 1
                dve.wait_ge(s["dve_step"], step[0])

            def layer_norm_stats():
                with dve.Fori(0, NT) as t:
                    v.bn_stats(st[:, ds(t, 1), :].rearrange("p a k -> p (a k)"),
                               xs[:, ds(t, 1), :].rearrange("p a d -> p (a d)")).then_inc(s["dve_step"], 1)
                step[0] += NT
                dve.wait_ge(s["dve_step"], step[0])
                link(v.tensor_tensor(mean[:], st[:, :, 1], st[:, :, 4], ALU.add))
                link(v.tensor_tensor(half_gap[:], st[:, :, 1], st[:, :, 4], ALU.subtract))
                link(v.tensor_tensor(rstd[:], st[:, :, 2], st[:, :, 5], ALU.add))
                link(v.tensor_scalar(mean[:], mean[:], 0.5, None, ALU.mult))
                link(v.tensor_tensor(half_gap[:], half_gap[:], half_gap[:], ALU.mult))
                link(v.tensor_scalar(rstd[:], rstd[:], 1.0 / D, EPS, ALU.mult, ALU.add))
                v.scalar_tensor_tensor(rstd[:], half_gap[:], 0.25, rstd[:], ALU.mult, ALU.add) \
                    .then_inc(s["stats_ready"], 1)

            def normalise(out, t):
                return v.tensor_scalar(out, xs[:, ds(t, 1), :].rearrange("p a d -> p (a d)"),
                                       mean[:, ds(t, 1)],
                                       rstd[:, ds(t, 1)], ALU.subtract, ALU.mult)

            dve.wait_ge(s["x_loaded"], 16)
            layer_norm_stats()
            dve.wait_ge(s["w_loaded"], W_SMALL)
            dve.wait_ge(s["consts_pool"], 4)
            link(v.tensor_scalar(keep[:], mask_i[:], 0.0, None, ALU.not_equal))
            link(v.tensor_scalar(mask_bias[0:S, :], mask_i[:], 0.0, MASKED, ALU.is_equal, ALU.mult))
            link(v.tensor_reduce(out=keep_any[:, 0:1], in_=keep[:], axis=AX, op=ALU.max))
            v.tensor_copy(keep_any[:, 1:P], keep_any[:, 0:1].broadcast_to([S, P - 1])) \
                .then_inc(s["consts_dve"], 1)
            link(v.tensor_reduce(out=local[:], in_=head_of[:].rearrange("p (g j) -> p j g", j=4), axis=AX,
                                 op=ALU.add))
            link(v.tensor_copy(diag[:, 1, :, :], local[:].unsqueeze(2).broadcast_to([P, 4, S])))
            dve.wait_ge(s["consts_mm"], 1)
            v.tensor_tensor(diag[:, 0, :, :], banks[7][:, 0:S].unsqueeze(1).broadcast_to([P, 4, S]),
                            diag[:, 1, :, :], ALU.mult).then_inc(s["consts_dve"], 1)
            dve.wait_ge(s["consts_dve"], 2)
            link(v.tensor_tensor(bcr[:], bcr[:], bdr[:], ALU.add))
            dve.wait_ge(s["rstd_ready"], 1)

            def xln_tile(t, u):
                if not isinstance(t, int) or t >= 2:
                    dve.wait_ge(s["tr_done"], t - 1)
                normalise(xln[:, u, :], t).then_inc(s["xln_ready"], 1)

            def values_evac(t, u):
                dve.wait_ge(s["proj_done"], t + 1)
                if not isinstance(t, int) or t >= 2:
                    dve.wait_ge(s["od_done"], 2 * (t - 1))
                v.tensor_tensor(vv[:, u, :].rearrange("p (b d) -> p b d", b=BT),
                                banks[7][:, 0:BT * D].rearrange("p (b d) -> p b d", b=BT),
                                bvr[:].unsqueeze(1).broadcast_to([P, BT, D]), ALU.add) \
                    .then_inc(s["v_evac"], 1)

            def max_and_shift(t, i, first):
                n = 4 * t + i
                dve.wait_ge(s["s_done"], n + 1)
                bank = banks[i % 2][:, :].rearrange("p (k t) -> p k t", k=4)
                v.tensor_reduce(out=nmax[:, i % 2, :], in_=bank, axis=AX, op=ALU.max, negate=True) \
                    .then_inc(s["nmax_ready"], 1)
                dve.wait_ge(s["nmax_ready"], n + 1)
                if not (first and i < 2):
                    dve.wait_ge(s["pt_done"], n - 1)
                v.tensor_tensor(pp[:, i % 2, :].rearrange("p (k t) -> p k t", k=4), bank,
                                nmax[:, i % 2, :].unsqueeze(2).broadcast_to([P, 4, T]), ALU.add) \
                    .then_inc(s["sub_done"], 1)

            def own_heads(t, u, b):
                m = 2 * t + b
                dve.wait_ge(s["od_done"], m + 1)
                if not isinstance(t, int) or m >= 1:
                    dve.wait_ge(s["od_summed"], m)
                v.tensor_tensor(od[:], banks[4][:, :], diag[:].rearrange("p w j s -> p (w j s)"), ALU.mult) \
                    .then_inc(s["od_read"], 1)
                dve.wait_ge(s["od_read"], m + 1)
                v.tensor_reduce(out=od_s[:, u, :, b, :], in_=od[:].rearrange("p (w j s) -> p w s j", w=2, j=4),
                                axis=AX, op=ALU.add).then_inc(s["od_summed"], 1)

            def attention_out(t, u):
                dve.wait_ge(s["od_summed"], 2 * t + 2)
                if not isinstance(t, int) or t >= 1:
                    dve.wait_ge(s["attn_ready"], t)
                v.reciprocal(rden[:], od_s[:, u, 1, :, :].rearrange("p b s -> p (b s)")) \
                    .then_inc(s["rden_ready"], 1)
                dve.wait_ge(s["rden_ready"], t + 1)
                v.tensor_tensor(attnT[:, u, :], od_s[:, u, 0, :, :].rearrange("p b s -> p (b s)"), rden[:],
                                ALU.mult).then_inc(s["attn_ready"], 1)

            def residual(t, u):
                xt = xs[:, ds(t, 1), :].rearrange("p a d -> p (a d)")
                v.tensor_tensor(xt, xt, bor[:], ALU.add).then_inc(s["xo_ready"], 1)
                dve.wait_ge(s["xo_ready"], t + 1)
                dve.wait_ge(s["wo_done"], t + 1)
                v.tensor_tensor(xt, banks[5][:, 0:D], xt, ALU.add).then_inc(s["x_updated"], 1)

            def tile(t, u, first, last):
                max_and_shift(t, 0, first)
                max_and_shift(t, 1, first)
                if not first:
                    own_heads(t - 1, 1 - u, 1)
                    attention_out(t - 1, 1 - u)
                max_and_shift(t, 2, first)
                if not last:
                    values_evac(t + 1, 1 - u)
                max_and_shift(t, 3, first)
                if not first:
                    residual(t - 1, 1 - u)
                if not (isinstance(t, int) and t + 2 >= NT):
                    xln_tile(t + 2, u)
                own_heads(t, u, 0)

            xln_tile(0, 0)
            xln_tile(1, 1)
            values_evac(0, 0)
            pairs_of_tiles(dve, tile, None, None)
            own_heads(NT - 1, 1, 1)
            attention_out(NT - 1, 1)
            residual(NT - 1, 1)
            dve.wait_ge(s["x_updated"], NT)

            layer_norm_stats()
            dve.wait_ge(s["rstd_ready"], 2)
            with dve.Fori(0, NT) as t:
                normalise(cur[:, ds(t, 1), :].rearrange("p a d -> p (a d)"), t).then_inc(s["ln_ready"], 1)
            for q in (1, 3):
                dve.wait_ge(s["t_done"], q + 1)
                v.tensor_copy(curT[:, q * 512:(q + 1) * 512], banks[q][:, :]).then_inc(s["t_evac"], 1)
            with dve.Fori(0, NT) as t:
                xt = xs[:, ds(t, 1), :].rearrange("p a d -> p (a d)")
                v.tensor_tensor(xt, xt, bcr[:], ALU.add).then_inc(s["dve_step"], 1)
            step[0] += NT
            dve.wait_ge(s["dve_step"], step[0])
            dve.wait_ge(s["scan_abs"], 1)
            link(v.tensor_scalar(sA[:], banks[4][:, :], bdl4[:, 0:1], 0.0, ALU.add, ALU.max))
            link(v.tensor_scalar(a_tmp[:, 3:4], a4[:], 0.0, None, ALU.max))
            dve.wait_ge(s["scan_soft"], 1)
            link(v.tensor_tensor(a4[:], a_tmp[:, 2:3], a_tmp[:, 3:4], ALU.add))
            link(v.tensor_tensor(sA[:], sA[:], sC[:], ALU.add))
            link(v.tensor_scalar(sB[:], sA[:], a4[:, 0:1], -1.0, ALU.mult, ALU.mult))
            link(v.tensor_tensor_scan(sD[:], not_first[:], sB[:], 0.0, ALU.mult, ALU.add))
            link(v.tensor_scalar(sD[:], sD[:], -20.0, 20.0, ALU.max, ALU.min))
            dve.wait_ge(s["scan_mm"], 2)
            link(v.scalar_tensor_tensor(sB[:], banks[5][:, :], bb4[:, 0:1], sA[:], ALU.add, ALU.mult))
            v.tensor_copy(a_tmp[:, 0:1], a_tmp[:, 0:1]).then_inc(s["scan_cum"], 1)
            dve.wait_ge(s["scan_exp"], 1)
            link(v.tensor_tensor(sB[:].rearrange("p (b t) -> p b t", t=S),
                                 sB[:].rearrange("p (b t) -> p b t", t=S), decay[:, :, 0:S], ALU.mult))
            link(v.tensor_tensor_scan(sC[:], not_first[:], sB[:], 0.0, ALU.mult, ALU.add))
            dve.wait_ge(s["scan_exp"], 2)
            v.tensor_tensor(sC[:], sC[:], sA[:], ALU.mult).then_inc(s["scan_h"], 1)
            for q in range(4):
                dve.wait_ge(s["scan_out"], q + 1)
                xq = xs[:, 4 * q:4 * q + 4, :].rearrange("p t d -> p (t d)")
                v.tensor_tensor(xq, banks[q][:, :], xq, ALU.add).then_inc(s["x2_ready"], 1)
            dve.wait_ge(s["x2_ready"], 4)
            layer_norm_stats()
            dve.wait_ge(s["rstd_ready"], 3)
            with dve.Fori(0, NT) as t:
                normalise(cur[:, ds(t, 1), :].rearrange("p a d -> p (a d)"), t).then_inc(s["ln_ready"], 1)

            base_steps = step[0]
            CHAIN = 37

            def one_layer(layer, parity, two):
                done = [0]

                def chain(ins):
                    ins.then_inc(s["dve_step"], 1)
                    done[0] += 1
                    dve.wait_ge(s["dve_step"], layer * CHAIN + (base_steps + done[0]))

                def ke(ap):
                    return ap.rearrange("p (k e) -> p k e", e=E)

                def over_e(ap):
                    return ap.unsqueeze(2).broadcast_to([P, NT, E])

                def over_k(ap):
                    return ap.unsqueeze(1).broadcast_to([P, NT, E])

                v.tensor_copy(rnow[:, 0:E], rt[:, ds(layer, 1), :].rearrange("p a e -> p (a e)")) \
                    .then_inc(s["router_ready"], 1)
                for q in (1, 3):
                    dve.wait_ge(s["t_done"], layer * 4 + (4 + q + 1))
                    v.tensor_copy(curT[:, q * 512:(q + 1) * 512], banks[q][:, :]).then_inc(s["t_evac"], 1)
                dve.wait_ge(s["logits_done"], layer + 1)
                v.tensor_copy(lgT[:], banks[4][:, :]).then_inc(s["lgT_ready"], 1)
                dve.wait_ge(s["lg_done"], layer + 1)
                chain(v.tensor_copy(
                    lg[:].rearrange("p (j c e) -> p j c e", j=4, c=4),
                    banks[5][:, :].rearrange("p (c j e) -> p j c e", c=4, j=4)[:, :, :, 0:E]))
                chain(v.tensor_reduce(out=mx[:], in_=ke(lg[:]), axis=AX, op=ALU.max))
                v.tensor_tensor(ke(ex[:]), ke(lg[:]), over_e(mx[:]), ALU.subtract).then_inc(s["sh_ready"], 1)
                dve.wait_ge(s["ex_ready"], layer + 1)
                chain(v.tensor_reduce(out=sm[:], in_=ke(ex[:]), axis=AX, op=ALU.add))
                chain(v.reciprocal(sm[:], sm[:]))
                chain(v.tensor_tensor(ke(pr[:]), ke(ex[:]), over_e(sm[:]), ALU.mult))
                chain(v.tensor_reduce(out=wt[:], in_=ke(pr[:]), axis=AX, op=ALU.max))
                chain(v.tensor_tensor(ke(eq[:]), ke(pr[:]), over_e(wt[:]), ALU.is_equal))
                chain(v.tensor_tensor(ke(eq[:]), ke(eq[:]), over_k(rev_e[:]), ALU.mult))
                chain(v.tensor_reduce(out=fm[:], in_=ke(eq[:]), axis=AX, op=ALU.max))
                v.tensor_tensor(ke(ohb[:]), ke(eq[:]), over_e(fm[:]), ALU.is_equal) \
                    .then_inc(s["oh_ready"], 1)
                chain(v.tensor_copy(wpart[:, 0, :], wt[:]))
                chain(v.tensor_tensor(wr[:], wt[:], wpart[:, 0, :], ALU.subtract))
                chain(v.tensor_copy(wpart[:, 1, :], wr[:]))
                chain(v.tensor_tensor(vals[:, :, 4], wr[:], wpart[:, 1, :], ALU.subtract))
                chain(v.tensor_copy(vals[:, :, 2:4].rearrange("p k w -> p w k"), wpart[:, 0:2, :]))
                dve.wait_ge(s["rank_mm"], layer + 1)
                chain(v.tensor_copy(tot[:].rearrange("p (e k) -> p e k", k=NT),
                                    banks[7][:, 0:256].rearrange("p (k e) -> p e k", e=E)))
                chain(v.tensor_tensor_scan(inc[:], not_first16[:], tot[:], 0.0, ALU.mult, ALU.add))
                chain(v.tensor_tensor(exc[:], inc[:], tot[:], ALU.subtract))
                chain(v.tensor_tensor(
                    ke(cmp[:]), inc[:].rearrange("p (e k) -> p e k", k=NT)[:, :, NT - 1:NT]
                    .broadcast_to([P, E, NT]), over_k(thr_gt[:]), ALU.is_gt))
                chain(v.tensor_reduce(out=nt[:], in_=ke(cmp[:]), axis=AX, op=ALU.add))
                chain(v.tensor_tensor_scan(itl[:], ones[:, 0:E], nt[:], 0.0, ALU.mult, ALU.add))
                chain(v.tensor_tensor(tb[:], itl[:], nt[:], ALU.subtract))
                chain(v.tensor_tensor(ke(rk[:]), ke(banks[6][:, 0:256]), exc[:].rearrange("p (e k) -> p k e", k=NT),
                                      ALU.add))
                chain(v.tensor_tensor(rk[:], rk[:], ohb[:], ALU.mult))
                chain(v.tensor_reduce(out=rank[:], in_=ke(rk[:]), axis=AX, op=ALU.add))
                chain(v.tensor_tensor(ke(cmp[:]), ke(ohb[:]), over_k(tb[:]), ALU.mult))
                chain(v.tensor_reduce(out=jb[:], in_=ke(cmp[:]), axis=AX, op=ALU.add))
                chain(v.tensor_tensor(ke(cmp[:]), over_e(rank[:]), over_k(thr_ge[:]), ALU.is_ge))
                chain(v.tensor_reduce(out=jo[:], in_=ke(cmp[:]), axis=AX, op=ALU.add))
                chain(v.tensor_tensor(jj[:], jb[:], jo[:], ALU.add))
                chain(v.scalar_tensor_tensor(rr[:], jo[:], -float(P), rank[:], ALU.mult, ALU.add))
                chain(v.tensor_tensor(ohj[:], iota_j[:].unsqueeze(1).broadcast_to([P, NT, SP2]),
                                      jj[:].unsqueeze(2).broadcast_to([P, NT, SP2]), ALU.is_equal))
                v.tensor_tensor(ohr[:], iota_r[:].unsqueeze(1).broadcast_to([P, NT, P]),
                                rr[:].unsqueeze(2).broadcast_to([P, NT, P]), ALU.is_equal)
                for n in range(NV):
                    last = v.tensor_tensor(carried[:, :, n, :], ohj[:],
                                           vals[:, :, n:n + 1].broadcast_to([P, NT, SP2]), ALU.mult)
                last.then_inc(s["inv_in"], 1)
                dve.wait_ge(s["inv_done"], layer + 1)
                chain(v.tensor_copy(inv[:].rearrange("p v j -> p (v j)"), banks[4][:, 0:NV * SP2]))
                v.tensor_scalar(pad[:], inv[:, 0, :], 0.0, None, ALU.is_equal)
                chain(v.scalar_tensor_tensor(tok[:], inv[:, 1, :], float(P), inv[:, 0, :], ALU.mult, ALU.add))
                v.tensor_scalar(gidx[:], tok[:], -1.0, 0.0, ALU.add, ALU.max)
                chain(v.tensor_tensor(pad[:], pad[:], dump_row[:], ALU.mult))
                v.scalar_tensor_tensor(sidx[:], tok[:], -1.0, pad[:], ALU.add, ALU.add)
                chain(v.tensor_tensor(wslot[:], inv[:, 2, :], inv[:, 3, :], ALU.add))
                v.tensor_tensor(wslot[:], wslot[:], inv[:, 4, :], ALU.add).then_inc(s["tables_ready"], 1)
                chain(v.tensor_tensor(scmp[:], iota_j[0:1, :].unsqueeze(2).broadcast_to([1, SP2, E]),
                                      itl[0:1, :].unsqueeze(1).broadcast_to([1, SP2, E]), ALU.is_ge))
                chain(v.tensor_reduce(out=sef[:], in_=scmp[:], axis=AX, op=ALU.add))
                v.tensor_scalar(slot_expert[:], sef[:], float(E - 1), None, ALU.min) \
                    .then_inc(s["expert_ready"], 1)
                assert done[0] == CHAIN, done

                def count(j):
                    return layer * SLOTS + j

                def step(i, u):
                    inner = not isinstance(i, int)
                    if has(i, 1, 7, 6):
                        j, p2 = i - 1, (u - 1) % 2
                        dve.wait_ge(s["tanh_done"], count(j + 1))
                        if inner or j >= 2:
                            dve.wait_ge(s["hT_mm"], count(j - 1))
                        v.scalar_tensor_tensor(hh[:, p2, :], th[:, p2, :], 1.0, banks[2 + p2][:, :],
                                               ALU.add, ALU.mult).then_inc(s["h_ready"], 1)
                    if has(i, 2, 7, 6):
                        j, p2 = i - 2, u % 2
                        dve.wait_ge(s["hT_mm"], count(j + 1))
                        if inner or j >= 2:
                            dve.wait_ge(s["y_mm"], count(j - 1))
                        v.tensor_copy(hT[:, p2, :], banks[4 + p2][:, :]).then_inc(s["hT_evac"], 1)
                    if has(i, 3, 7, 6):
                        j, p2, p4 = i - 3, (u - 3) % 2, (u - 3) % 4
                        dve.wait_ge(s["y_mm"], count(j + 1))
                        if inner or j >= 4:
                            dve.wait_ge(scattered[p4], scatter_count(layer, j - 4, p4))
                        v.tensor_scalar(yout[:, p4, :], banks[6 + p2][:, 0:D], wslot[:, ds(j, 1)], 0.5,
                                        ALU.mult, ALU.mult).then_inc(s["y_ready"], 1)

                slot_steps(dve, step, 3, 7, 6)

            layers(dve, one_layer)
            dve.wait_ge(s["cur_loaded"], (L + 1) * 16)
            for half in range(2):
                a = slice(half * NT // 2, (half + 1) * NT // 2)
                v.tensor_tensor(xs[:, a, :], xs[:, a, :], cur[:, a, :], ALU.add).then_inc(s["out_ready"], 1)


_INS = ['x', 'ctx_1024', 'mask_SxS2_ik0', 'L0_xattn_Wq', 'L0_xattn_bq', 'L0_xattn_Wk', 'L0_xattn_bk',
        'L0_xattn_Wv', 'L0_xattn_bv', 'L0_xattn_Wo', 'L0_xattn_bo', 'L0_attn_A', 'L0_attn_Wb',
        'L0_attn_bb', 'L0_attn_Wc', 'L0_attn_bc', 'L0_attn_Wd', 'L0_attn_bd', 'L0_attn_Wdelta',
        'L0_attn_bdelta', 'L0_ffn_routers', 'L0_ffn_W1', 'L0_ffn_W2']


def kernel(**inputs):
    import numpy as _np
    import concourse.bacc as _bacc
    from concourse import mybir as _mybir
    from concourse.bass_utils import run_bass_kernel_spmd as _run

    nc = _bacc.Bacc("TRN2", target_bir_lowering=False, num_devices=1)
    arrays, args = {}, []
    for name in _INS:
        a = _np.ascontiguousarray(inputs[name])
        arrays[f"in_{name}_dram"] = a
        args.append(nc.dram_tensor(f"in_{name}_dram", a.shape, _mybir.dt.from_np(a.dtype), kind="ExternalInput").ap())
    shape = inputs["x"].shape
    args.append(nc.dram_tensor("out_0_dram", shape, _mybir.dt.from_np(_np.dtype("float32")), kind="ExternalOutput").ap())
    perceiver_block(nc, *args)
    r = _run(nc, [arrays], core_ids=[0])
    return r.results[0]["out_0_dram"]
```

```python
from contextlib import ExitStack

import concourse.bass as bass
from concourse import mybir

P = 128
F32 = mybir.dt.float32
BF16 = mybir.dt.bfloat16
I32 = mybir.dt.int32
ACT = mybir.ActivationFunctionType
ALU = mybir.AluOpType
AX = mybir.AxisListType.X

EPS = 1e-5
MASKED = -1e30
HEADS = 16


def ds(start, size):
    return bass.ds(start, size)


def perceiver_block(nc, x, ctx, mask, Wq, bq, Wk, bk, Wv, bv, Wo, bo, A, Wb, bb, Wc, bc, Wd, bd,
                    Wdelta, bdelta, routers, W1, W2, out):
    B, S, D = x.shape
    T = ctx.shape[1]
    HD = D // HEADS
    H = A.shape[0]
    L, _, E = routers.shape
    FF = W1.shape[2]
    N = B * S
    NT = N // P
    BT = P // S
    NG = P // H
    GT = NT // NG
    GW = GT * P
    SLOTS = NT + E - 1
    SP2 = 32
    FC = FF // P
    PAIRS = HEADS // 2
    NV = 5
    DUMP = N
    ROWS = N + SP2 * P
    assert D == P and T == P and S * 2 == P and NG == 4 and E == 16 and L % 2 == 0

    x_t = x.rearrange("b s d -> (b s) d").rearrange("(t p) d -> p t d", p=P)
    out_t = out.rearrange("b s d -> (b s) d").rearrange("(t p) d -> p t d", p=P)
    ctx_t = ctx.rearrange("b t d -> t b d")
    rows = [nc.dram_tensor(f"token_rows_{i}", (ROWS, D), F32, kind="Internal").ap() for i in range(2)]

    def col(v):
        return v.rearrange("(n a) -> n a", a=1)

    with ExitStack() as stack:
        def sb(name, shape, dt=F32):
            return stack.enter_context(nc.sbuf_tensor(name, shape, dt))

        def sem(name):
            return stack.enter_context(nc.semaphore(name))

        banks = [stack.enter_context(nc.psum_tensor(f"bank{i}", [P, 512], F32)) for i in range(8)]

        wq, wk, wv, wo, wd = (sb(n, [P, D]) for n in ("wq", "wk", "wv", "wo", "wd"))
        wdl, wb = sb("wdl", [D, H]), sb("wb", [D, H])
        wc_own = sb("wc_own", [P, NG, D])
        w1 = sb("w1", [P, E * FF])
        w2 = sb("w2", [P, E * FF])
        rt = sb("rt", [P, L, E])
        rnow = sb("rnow", [P, 32])
        bqc, bkc = sb("bqc", [P, 1]), sb("bkc", [P, 1])
        bvr, bor, bcr, bdr = (sb(n, [P, D]) for n in ("bvr", "bor", "bcr", "bdr"))
        bdl4, bb4, a4 = sb("bdl4", [P, 1]), sb("bb4", [P, 1]), sb("a4", [P, 1])
        a_tmp = sb("a_tmp", [P, 4])
        ident = sb("ident", [P, P])
        ones = sb("ones", [P, P])
        onesb = sb("onesb", [P, P], BF16)
        trib = sb("trib", [P, P], BF16)
        pair_rows = sb("pair_rows", [P, P], BF16)
        mask_i = sb("mask_i", [S, T], I32)
        mask_bias = sb("mask_bias", [P, T], BF16)
        keep = sb("keep", [S, T])
        keep_any = sb("keep_any", [S, P])
        head_of = sb("head_of", [P, HEADS])
        local = sb("local", [P, 4])
        diag = sb("diag", [P, 2, 4, S])
        iota_r = sb("iota_r", [P, P])
        thr_gt = sb("thr_gt", [P, 16])
        iota_j = sb("iota_j", [P, SP2])
        dump_row = sb("dump_row", [P, SP2])
        not_first = sb("not_first", [P, GW])
        not_first16 = sb("not_first16", [P, 256])
        vals = sb("vals", [P, NT, NV], BF16)
        xs = sb("xs", [P, NT, D])
        cur = sb("cur", [P, NT, D])
        curT = sb("curT", [P, N])
        st = sb("st", [P, NT, 6])
        mean = sb("mean", [P, NT])
        half_gap = sb("half_gap", [P, NT])
        rstd = sb("rstd", [P, NT])
        xln = sb("xln", [P, 2, D])
        cx = sb("cx", [P, 2, BT, D])
        aT = sb("aT", [P, 2, 3 * P])
        qT = sb("qT", [P, 2, P])
        qm = sb("qm", [P, 2, BT * HEADS * S])
        kT = sb("kT", [P, 2, BT * T])
        vv = sb("vv", [P, 2, BT * D])
        nmax = sb("nmax", [P, 2, 4])
        pp = sb("pp", [P, 2, 512])
        ppT = sb("ppT", [P, 4, 512])
        od = sb("od", [P, 512])
        od_s = sb("od_s", [P, 2, 2, BT, S])
        rden = sb("rden", [P, BT * S])
        attnT = sb("attnT", [P, 2, P])
        sA, sB, sC, sD = (sb(n, [P, GW]) for n in ("sA", "sB", "sC", "sD"))
        decay = sb("decay", [P, GW // S, S + 1])
        lgT = sb("lgT", [P, 512])
        lg, ex, pr, eq, nth, cmp, rk = (sb(n, [P, 256]) for n in ("lg", "ex", "pr", "eq", "nth", "cmp", "rk"))
        ohb = sb("ohb", [P, 256], BF16)
        mx, sm, wt, nt, itl, tb, place, wr = (sb(n, [P, 16]) for n in
                                              ("mx", "sm", "wt", "nt", "itl", "tb", "place", "wr"))
        place_i, row_i, slot_i = (sb(n, [P, NT], I32) for n in ("place_i", "row_i", "slot_i"))
        ohr = sb("ohr", [P, NT, P], BF16)
        ohj = sb("ohj", [P, NT, SP2], BF16)
        carried = sb("carried", [P, NT, NV, SP2], BF16)
        pad = sb("pad", [P, SP2])
        tok = sb("tok", [P, SP2])
        wslot = sb("wslot", [P, SP2])
        gidx = sb("gidx", [P, SP2], I32)
        sidx = sb("sidx", [P, SP2], I32)
        scmp = sb("scmp", [1, SP2, E])
        sef = sb("sef", [1, SP2])
        slot_expert = sb("slot_expert", [1, SP2], I32)
        xin = sb("xin", [P, 4, D])
        yout = sb("yout", [P, 4, D])
        xT = sb("xT", [P, 2, P])
        th = sb("th", [P, 2, FF])
        hh = sb("hh", [P, 2, FF])
        w1_slot = sb("w1_slot", [P, 2, FF])

        names = """x_loaded w_loaded later_loaded w1_loaded w2_loaded stored rows_stored
            consts_pool consts_dve consts_mm dve_step act_step
            stats_ready rstd_ready ln_ready
            xln_ready tr_done a_evac proj_done q_evac k_evac v_evac qm_ready s_done exp_done
            pt_done pt_evac od_done od_read attn_ready wo_done x_updated x_stats xb_ready
            t_done t_evac scan_mm scan_abs scan_soft scan_cum scan_exp scan_h scan_out x2_ready
            router_ready logits_done lgT_ready lg_done sh_ready ex_ready oh_ready rank_mm
            slots_hot carried_ready inv_in inv_done gidx_ready expert_ready
            nmax_ready od_summed rden_ready xo_ready
            waited_alone xT_mm xT_evac w1_staged h_mm tanh_done h_ready y_mm y_ready
            out_ready""".split()
        s = dict(zip(names, [sem(n) for n in names]))
        ctx_loaded = [sem(f"ctx_loaded{u}") for u in range(2)]
        gathered = [sem(f"gathered{u}") for u in range(4)]
        scattered = [sem(f"scattered{u}") for u in range(4)]
        cur_loaded = [sem(f"cur_loaded{q}") for q in range(4)]
        per_u = [len(range(u, SLOTS, 4)) for u in range(4)]

        attention_weights = [
            (wk[:], Wk), (wv[:], Wv), (wq[:], Wq), (mask_i[:], mask), (bqc[:], col(bq)), (bkc[:], col(bk)),
            (bvr[:], bv.partition_broadcast(P)), (wo[:], Wo), (bor[:], bo.partition_broadcast(P))]
        later_weights = [
            (wdl[:], Wdelta), (wb[:], Wb), (wd[:], Wd), (rt[:], routers.rearrange("l d e -> d l e")),
            (bcr[:], bc.partition_broadcast(P)), (bdr[:], bd.partition_broadcast(P))]
        later_weights += [(dst[g * H:(g + 1) * H, :], src) for g in range(NG)
                          for dst, src in ((wc_own[:, g, :], Wc), (bdl4, col(bdelta)), (bb4, col(bb)),
                                           (a4, col(A)))]
        W_ATT = 16 * len(attention_weights)
        W_LATER = 16 * len(later_weights)

        def pairs_of_tiles(eng, body, first, last):
            body(0, 0, first=True, last=False)
            body(1, 1, first=False, last=False)
            with eng.Fori(2, NT - 3, 2) as t:
                body(t, 0, first=False, last=False)
                body(t + 1, 1, first=False, last=False)
            body(NT - 2, 0, first=False, last=False)
            body(NT - 1, 1, first=False, last=True)

        def layers(eng, body):
            with eng.Fori(0, L // 2) as two:
                for parity in range(2):
                    body(two * 2 + parity, parity, two)

        def slot_steps(eng, step, depth, lo=7, loops=6):
            for i in range(lo):
                step(i, i % 4)
            with eng.Fori(lo, lo + 4 * loops - 3, 4) as i:
                for k in range(4):
                    step(i + k, (lo + k) % 4)
            for i in range(lo + 4 * loops, SLOTS + depth):
                step(i, i % 4)

        def has(i, lag):
            return not isinstance(i, int) or 0 <= i - lag < SLOTS

        def expert_of(slot, engine):
            return nc.values_load(
                slot_expert[0:1, ds(slot, 1)], engines=[engine], min_val=0, max_val=E - 1,
                skip_runtime_bounds_check_because="the vector engine bounds it by E - 1")

        def wait_alone(eng, which, value):
            eng.wait_ge(which, value)
            eng.sem_inc(s["waited_alone"], 1)

        block = stack.enter_context(nc.Block())

        @block.sync
        def _(sp):
            sp.dma_start(xs[:], x_t).then_inc(s["x_loaded"], 16)
            def load_ctx(t, u, first, last):
                if not isinstance(t, int) or t >= 2:
                    wait_alone(sp, s["tr_done"], t - 1)
                sp.dma_start(cx[:, u, :, :], ctx_t[:, ds(t * BT, BT), :]).then_inc(ctx_loaded[u], 16)

            load_ctx(0, 0, True, False)
            for dst, src in attention_weights:
                sp.dma_start(dst, src).then_inc(s["w_loaded"], 16)
            load_ctx(1, 1, True, False)
            sp.wait_ge(s["consts_pool"], 1)
            for dst, src in later_weights:
                sp.dma_start(dst, src).then_inc(s["later_loaded"], 16)
            with sp.Fori(2, NT - 1, 2) as t:
                load_ctx(t, 0, False, False)
                load_ctx(t + 1, 1, False, False)
            sp.dma_start(w1[:].rearrange("p (e f) -> p e f", e=E), W1.rearrange("e d f -> d e f")) \
                .then_inc(s["w1_loaded"], 16)
            sp.dma_start(w2[:].rearrange("p (e c d) -> p e c d", e=E, c=FC),
                         W2.rearrange("e (c p) d -> p e c d", p=P)).then_inc(s["w2_loaded"], 16)
            sp.wait_ge(s["ln_ready"], 2 * NT)
            sp.dma_start(rows[0][0:N, :].rearrange("(t p) d -> p t d", p=P), cur[:]) \
                .then_inc(s["rows_stored"], 16)
            for q in range(4):
                sp.sem_inc(cur_loaded[q], 16)

            def load_next(layer, source):
                wait_alone(sp, s["t_done"], (layer + 2) * 4)
                for u in range(4):
                    wait_alone(sp, scattered[u], (layer + 1) * (16 * per_u[u]))
                for q in range(4):
                    sp.dma_start(cur[:, 4 * q:4 * q + 4, :],
                                 source[q * 4 * P:(q + 1) * 4 * P, :].rearrange("(t p) d -> p t d", p=P)) \
                        .then_inc(cur_loaded[q], 16)

            with sp.Fori(0, L // 2) as two:
                load_next(two * 2, rows[1])
                load_next(two * 2 + 1, rows[0])
            for q in range(4):
                sp.wait_ge(s["out_ready"], q + 1)
                sp.dma_start(out_t[:, 4 * q:4 * q + 4, :], xs[:, 4 * q:4 * q + 4, :]).then_inc(s["stored"], 16)
            sp.wait_ge(s["rows_stored"], 16)
            sp.wait_ge(s["stored"], 64)

        @block.gpsimd
        def _(pool):
            g = nc.gpsimd
            g.memset(ident[:], 0.0)
            g.memset(ones[:], 1.0)
            g.memset(onesb[:], 1.0)
            g.memset(head_of[:], 1.0)
            g.memset(mask_bias[:], 0.0)
            g.memset(rnow[:], 0.0)
            g.memset(wc_own[:], 0.0)
            g.memset(not_first[:], 1.0)
            g.memset(not_first16[:], 1.0)
            g.memset(decay[:], 1.0).then_inc(s["consts_pool"], 1)
            for dst, pat, base, cm in [
                    (iota_r[:], [[1, P]], 0, 0),
                    (thr_gt[:], [[P, 16]], 0, 0), (iota_j[:], [[1, SP2]], 0, 0),
                    (dump_row[:], [[P, SP2]], DUMP + 1, 1),
                    (vals[:, :, 0], [[0, NT]], 1, 1), (vals[:, :, 1], [[1, NT]], 0, 0)]:
                last = g.iota(dst, pattern=pat, base=base, channel_multiplier=cm,
                              allow_small_or_imprecise_dtypes=True)
            last.then_inc(s["consts_pool"], 1)
            pool.wait_ge(s["consts_pool"], 2)
            g.affine_select(out=ident[:], in_=ident[:], compare_op=ALU.not_equal, fill=1.0, base=0,
                            pattern=[[-1, P]], channel_multiplier=1)
            g.affine_select(out=trib[:], in_=onesb[:], compare_op=ALU.is_gt, fill=0.0, base=0,
                            pattern=[[1, P]], channel_multiplier=-1)
            g.affine_select(out=head_of[:], in_=head_of[:], compare_op=ALU.is_ge, fill=0.0, base=0,
                            pattern=[[-HD, HEADS]], channel_multiplier=1).then_inc(s["consts_pool"], 1)
            pool.wait_ge(s["consts_pool"], 3)
            g.affine_select(out=head_of[:], in_=head_of[:], compare_op=ALU.is_ge, fill=0.0, base=HD - 1,
                            pattern=[[HD, HEADS]], channel_multiplier=-1)
            nf = not_first[:].rearrange("p (b t) -> p b t", t=S)
            g.memset(nf[:, :, 0:1], 0.0)
            nf16 = not_first16[:].rearrange("p (e k) -> p e k", k=NT)
            g.memset(nf16[:, :, 0:1], 0.0)
            g.tensor_copy(pair_rows[:, 0:S], ident[:, 0:S])
            g.tensor_copy(pair_rows[:, S:P], ident[:, 0:S]).then_inc(s["consts_pool"], 1)

            def masked_queries(t, u, first, last):
                pool.wait_ge(s["q_evac"], t + 1)
                if not isinstance(t, int) or t >= 2:
                    pool.wait_ge(s["s_done"], 4 * (t - 1))
                for b in range(BT):
                    w = HEADS * S
                    g.tensor_tensor(
                        qm[:, u, b * w:(b + 1) * w].rearrange("p (h s) -> p h s", h=HEADS),
                        qT[:, u, b * S:(b + 1) * S].unsqueeze(1).broadcast_to([P, HEADS, S]),
                        head_of[:].unsqueeze(2).broadcast_to([P, HEADS, S]), ALU.mult) \
                        .then_inc(s["qm_ready"], 1)

            pairs_of_tiles(pool, masked_queries, None, None)
            pool.wait_ge(s["ln_ready"], NT)
            g.tensor_tensor(xs[:], xs[:], bcr[:].unsqueeze(1).broadcast_to([P, NT, D]), ALU.add) \
                .then_inc(s["xb_ready"], 1)

            pool.wait_ge(s["rows_stored"], 16)

            LAG = 6

            def one_layer(layer, parity, two):
                src, dst = rows[parity], rows[1 - parity]
                wait_alone(pool, s["slots_hot"], layer + 1)
                for n in range(1, NV):
                    last = g.tensor_tensor(carried[:, :, n, :], ohj[:],
                                           vals[:, :, n:n + 1].broadcast_to([P, NT, SP2]), ALU.mult)
                last.then_inc(s["carried_ready"], 1)
                wait_alone(pool, s["gidx_ready"], layer + 1)
                for i in range(SLOTS + LAG):
                    if i < SLOTS:
                        if i >= 4:
                            wait_alone(pool, s["xT_mm"], layer * SLOTS + (i - 3))
                        g.indirect_dma_start(
                            out=xin[:, i % 4, :], out_offset=None, in_=src[0:N, :],
                            in_offset=bass.IndirectOffsetOnAxis(ap=gidx[:, i:i + 1], axis=0)) \
                            .then_inc(gathered[i % 4], 16)
                    if i >= LAG:
                        j = i - LAG
                        wait_alone(pool, s["y_ready"], layer * SLOTS + (j + 1))
                        g.indirect_dma_start(
                            out=dst, out_offset=bass.IndirectOffsetOnAxis(ap=sidx[:, j:j + 1], axis=0),
                            in_=yout[:, j % 4, :], in_offset=None).then_inc(scattered[j % 4], 16)

            layers(pool, one_layer)

        def scatter_count(layer, j, v):
            return layer * (16 * per_u[v]) + (j - v) * 4 + 16

        @block.scalar
        def _(act):
            a = nc.scalar
            def rstd_of(n):
                act.wait_ge(s["stats_ready"], n)
                a.activation(rstd[:], rstd[:], ACT.Ln).then_inc(s["act_step"], 1)
                step[0] += 1
                act.wait_ge(s["act_step"], step[0])
                a.activation(rstd[:], rstd[:], ACT.Exp, scale=-0.5).then_inc(s["rstd_ready"], 1)

            step = [0]
            rstd_of(1)
            act.wait_ge(s["w_loaded"], W_ATT)
            a.mul(bqc[:], bqc[:], float(HD) ** -0.5).then_inc(s["act_step"], 1)
            step[0] += 1
            act.wait_ge(s["act_step"], step[0])

            def evac_inputs(t, u):
                act.wait_ge(s["tr_done"], t + 1)
                if not isinstance(t, int) or t >= 2:
                    act.wait_ge(s["proj_done"], t - 1)
                a.copy(aT[:, u, :], banks[5][:, 0:3 * P]).then_inc(s["a_evac"], 1)

            def evac_qk(t, u):
                act.wait_ge(s["proj_done"], t + 1)
                if not isinstance(t, int) or t >= 2:
                    act.wait_ge(s["qm_ready"], 2 * (t - 1))
                    act.wait_ge(s["s_done"], 4 * (t - 1))
                a.activation(qT[:, u, :], banks[6][:, 0:P], ACT.Identity, bias=bqc[:, 0:1],
                             scale=float(HD) ** -0.5).then_inc(s["q_evac"], 1)
                a.activation(kT[:, u, :], banks[6][:, P:3 * P], ACT.Identity, bias=bkc[:, 0:1],
                             scale=1.0).then_inc(s["k_evac"], 1)

            def exp_scores(t, i, first):
                n = 4 * t + i
                act.wait_ge(s["nmax_ready"], n + 1)
                if not (first and i < 2):
                    act.wait_ge(s["pt_done"], n - 1)
                for k in range(4):
                    last = a.activation(pp[:, i % 2, k * T:(k + 1) * T], banks[i % 2][:, k * T:(k + 1) * T],
                                        ACT.Exp, bias=nmax[:, i % 2, k:k + 1], scale=1.0)
                last.then_inc(s["exp_done"], 1)

            def evac_pt(t, i):
                n = 4 * t + i
                act.wait_ge(s["pt_done"], n + 1)
                if not isinstance(t, int) or t >= 1:
                    act.wait_ge(s["od_done"], 2 * t + (i // 2 - 1))
                a.copy(ppT[:, i, :], banks[2 + i % 2][:, :]).then_inc(s["pt_evac"], 1)

            def tile(t, u, first, last):
                if not first:
                    evac_pt(t - 1, 2)
                exp_scores(t, 0, first)
                if not first:
                    evac_pt(t - 1, 3)
                if not last:
                    evac_qk(t + 1, 1 - u)
                exp_scores(t, 1, first)
                evac_pt(t, 0)
                if not (isinstance(t, int) and t + 2 >= NT):
                    evac_inputs(t + 2, u)
                exp_scores(t, 2, first)
                evac_pt(t, 1)
                exp_scores(t, 3, first)

            evac_inputs(0, 0)
            evac_inputs(1, 1)
            evac_qk(0, 0)
            pairs_of_tiles(act, tile, None, None)
            evac_pt(NT - 1, 2)
            evac_pt(NT - 1, 3)

            def evac_tiles(done, first_dve):
                for q in (0, 2):
                    act.wait_ge(s["t_done"], done + q + 1)
                    a.copy(curT[:, q * 512:(q + 1) * 512], banks[q][:, :]).then_inc(s["t_evac"], 1)

            rstd_of(2)
            evac_tiles(0, None)
            act.wait_ge(s["later_loaded"], W_LATER)
            a.activation(a_tmp[:, 0:1], a4[:], ACT.Abs)
            act.wait_ge(s["scan_mm"], 1)
            a.activation(sC[:], banks[4][:, :], ACT.Abs, bias=bdl4[:, 0:1]).then_inc(s["scan_abs"], 1)
            act.wait_ge(s["scan_abs"], 1)
            a.activation(sC[:], sC[:], ACT.Exp, scale=-1.0)
            a.activation(a_tmp[:, 1:2], a_tmp[:, 0:1], ACT.Exp, scale=-1.0).then_inc(s["act_step"], 1)
            step[0] += 1
            act.wait_ge(s["act_step"], step[0])
            a.activation(sC[:], sC[:], ACT.Ln, bias=1.0)
            a.activation(a_tmp[:, 2:3], a_tmp[:, 1:2], ACT.Ln, bias=1.0).then_inc(s["scan_soft"], 1)
            act.wait_ge(s["scan_cum"], 1)
            a.activation(decay[:, :, 1:S + 1], sD[:].rearrange("p (b t) -> p b t", t=S), ACT.Exp,
                         scale=-1.0).then_inc(s["scan_exp"], 1)
            a.activation(sA[:], sD[:], ACT.Exp).then_inc(s["scan_exp"], 1)
            rstd_of(3)

            def one_layer(layer, parity, two):
                done = layer * 4 + 4
                for q in (0, 2):
                    act.wait_ge(s["t_done"], done + (q + 1))
                    a.copy(curT[:, q * 512:(q + 1) * 512], banks[q][:, :]).then_inc(s["t_evac"], 1)
                act.wait_ge(s["sh_ready"], layer + 1)
                a.activation(ex[:], ex[:], ACT.Exp).then_inc(s["ex_ready"], 1)

                wait_alone(act, s["expert_ready"], layer + 1)

                def step(i, u):
                    inner = not isinstance(i, int)
                    if has(i, 0):
                        e = expert_of(i, mybir.EngineType.Activation)
                        act.wait_ge(s["xT_mm"], layer * SLOTS + (i + 1))
                        if inner or i >= 2:
                            act.wait_ge(s["h_mm"], layer * SLOTS + (i - 1))
                        a.copy(xT[:, u % 2, :], banks[u % 2][:, 0:P]).then_inc(s["xT_evac"], 1)
                        a.copy(w1_slot[:, u % 2, :], w1[:, ds(e * FF, FF)]).then_inc(s["w1_staged"], 1)
                    if has(i, 1):
                        j, v = i - 1, (u - 1) % 2
                        act.wait_ge(s["h_mm"], layer * SLOTS + (j + 1))
                        if inner or j >= 2:
                            act.wait_ge(s["h_ready"], layer * SLOTS + (j - 1))
                        a.activation(th[:, v, :], banks[2 + v][:, :], ACT.Tanh, scale=0.5) \
                            .then_inc(s["tanh_done"], 1)

                slot_steps(act, step, 2)

            layers(act, one_layer)

        @block.tensor
        def _(pe):
            mm = nc.tensor.matmul
            pe.wait_ge(s["consts_pool"], 4)

            def transposes_in(t, u):
                pe.wait_ge(s["xln_ready"], t + 1)
                pe.wait_ge(ctx_loaded[u], (t - u) * 8 + 16)
                if not isinstance(t, int) or t >= 1:
                    pe.wait_ge(s["a_evac"], t)
                nc.tensor.transpose(banks[5][:, 0:P], xln[:, u, :], ident[:])
                nc.tensor.transpose(banks[5][:, P:2 * P], cx[:, u, 0, :], ident[:])
                nc.tensor.transpose(banks[5][:, 2 * P:3 * P], cx[:, u, 1, :], ident[:]) \
                    .then_inc(s["tr_done"], 1)

            def project(t, u):
                pe.wait_ge(s["a_evac"], t + 1)
                if not isinstance(t, int) or t >= 1:
                    pe.wait_ge(s["k_evac"], t)
                    pe.wait_ge(s["v_evac"], t)
                for b in range(BT):
                    mm(banks[7][:, b * D:(b + 1) * D], aT[:, u, (1 + b) * P:(2 + b) * P], wv[:],
                       start=True, stop=True)
                mm(banks[6][:, 0:P], wq[:], aT[:, u, 0:P], start=True, stop=True)
                mm(banks[6][:, P:3 * P], wk[:], aT[:, u, P:3 * P], start=True, stop=True) \
                    .then_inc(s["proj_done"], 1)

            def scores(t, u, i, first):
                n = 4 * t + i
                b, half = i // 2, i % 2
                if half == 0:
                    pe.wait_ge(s["qm_ready"], 2 * t + (b + 1))
                if i == 0:
                    pe.wait_ge(s["k_evac"], t + 1)
                if not (first and i < 2):
                    pe.wait_ge(s["exp_done"], n - 1)
                bank = banks[i % 2]
                mm(bank[:, :].rearrange("p (k t) -> p k t", k=4), pair_rows[:],
                   mask_bias[:].unsqueeze(1).broadcast_to([P, 4, T]), start=True, stop=False)
                for k in range(4):
                    c = ((b * HEADS) + (half * 4 + k) * 2) * S
                    last = mm(bank[:, k * T:(k + 1) * T], qm[:, u, c:c + P], kT[:, u, b * T:(b + 1) * T],
                              start=False, stop=(k == 3))
                last.then_inc(s["s_done"], 1)

            def transpose_probs(n, i4, early):
                pe.wait_ge(s["exp_done"], n + 1)
                if not early:
                    pe.wait_ge(s["pt_evac"], n - 1)
                for k in range(4):
                    last = nc.tensor.transpose(banks[2 + i4 % 2][:, k * P:(k + 1) * P],
                                               pp[:, i4 % 2, k * P:(k + 1) * P], ident[:])
                last.then_inc(s["pt_done"], 1)

            def values(t, u, b, early):
                pe.wait_ge(s["pt_evac"], 4 * t + 2 * b + 2)
                if b == 0:
                    pe.wait_ge(s["v_evac"], t + 1)
                if not early:
                    if b == 0:
                        pe.wait_ge(s["x_updated"], t)
                    else:
                        pe.wait_ge(s["od_read"], 2 * t + 1)
                for which in range(2):
                    for g in range(4):
                        lhsT = vv[:, u, b * D + 32 * g:b * D + 32 * g + 32] if which == 0 else ones[:, 0:32]
                        src = ppT[:, 2 * b + g // 2, (g % 2) * 256:(g % 2) * 256 + 256]
                        last = mm(banks[4][32 * g:32 * g + 32, which * 256:(which + 1) * 256], lhsT, src,
                                  start=True, stop=True)
                last.then_inc(s["od_done"], 1)

            def project_out(t, u):
                pe.wait_ge(s["attn_ready"], t + 1)
                mm(banks[4][:, 0:D], attnT[:, u, :], wo[:], start=True, stop=True).then_inc(s["wo_done"], 1)

            def tile(t, u, first, last):
                n = 4 * t
                again = isinstance(t, int) and t == 1
                scores(t, u, 0, first)
                if not first:
                    transpose_probs(n - 2, 2, False)
                    values(t - 1, 1 - u, 0, again)
                if not last:
                    project(t + 1, 1 - u)
                if not first:
                    transpose_probs(n - 1, 3, False)
                scores(t, u, 1, first)
                if not first:
                    values(t - 1, 1 - u, 1, False)
                scores(t, u, 2, False)
                transpose_probs(n, 0, first)
                if not (isinstance(t, int) and t + 2 >= NT):
                    transposes_in(t + 2, u)
                scores(t, u, 3, False)
                transpose_probs(n + 1, 1, first)
                if not first:
                    project_out(t - 1, 1 - u)

            transposes_in(0, 0)
            transposes_in(1, 1)
            pe.wait_ge(s["w_loaded"], W_ATT)
            project(0, 0)
            pe.wait_ge(s["consts_dve"], 1)
            mm(banks[4][:, 0:S], keep_any[:, :], ident[0:S, 0:S], start=True, stop=True) \
                .then_inc(s["consts_mm"], 1)
            pe.wait_ge(s["consts_dve"], 2)
            pairs_of_tiles(pe, tile, None, None)
            transpose_probs(4 * NT - 2, 2, False)
            values(NT - 1, 1, 0, False)
            transpose_probs(4 * NT - 1, 3, False)
            values(NT - 1, 1, 1, False)
            project_out(NT - 1, 1)

            def transpose_tiles(loaded=None):
                for q in range(4):
                    if loaded is not None:
                        pe.wait_ge(cur_loaded[q], loaded)
                    for k in range(4):
                        last = nc.tensor.transpose(banks[q][:, k * P:(k + 1) * P], cur[:, 4 * q + k, :],
                                                   ident[:])
                    last.then_inc(s["t_done"], 1)

            pe.wait_ge(s["ln_ready"], NT)
            transpose_tiles()
            pe.wait_ge(s["t_evac"], 4)
            pe.wait_ge(s["later_loaded"], W_LATER)
            for w, bank in ((wdl, banks[4]), (wb, banks[5])):
                for g in range(NG):
                    last = mm(bank[H * g:H * (g + 1), :], w[:], curT[:, g * GW:(g + 1) * GW],
                              start=True, stop=True)
                last.then_inc(s["scan_mm"], 1)
            for k in range(NT):
                mm(banks[k // 4][:, (k % 4) * P:(k % 4 + 1) * P], curT[:, k * P:(k + 1) * P], wd[:],
                   start=(k % 4 == 0), stop=False)
            pe.wait_ge(s["scan_h"], 1)
            for k in range(NT):
                g, c = k // GT, k % GT
                last = mm(banks[k // 4][:, (k % 4) * P:(k % 4 + 1) * P], sC[:, c * P:(c + 1) * P],
                          wc_own[:, g, :], start=False, stop=(k % 4 == 3))
                if k % 4 == 3:
                    last.then_inc(s["scan_out"], 1)

            pe.wait_ge(s["w1_loaded"], 16)
            pe.wait_ge(s["w2_loaded"], 16)
            pe.wait_ge(s["x2_ready"], 4)

            def one_layer(layer, parity, two):
                transpose_tiles((layer + 1) * 16)
                pe.wait_ge(s["t_evac"], layer * 4 + 8)
                pe.wait_ge(s["router_ready"], layer + 1)
                for g in range(4):
                    last = mm(banks[4][32 * g:32 * g + 32, :], rnow[:], curT[:, g * 512:(g + 1) * 512],
                              start=True, stop=True)
                last.then_inc(s["logits_done"], 1)
                pe.wait_ge(s["lgT_ready"], layer + 1)
                for c in range(4):
                    last = nc.tensor.transpose(banks[5][:, c * P:(c + 1) * P], lgT[:, c * P:(c + 1) * P],
                                               ident[:])
                last.then_inc(s["lg_done"], 1)
                pe.wait_ge(s["oh_ready"], layer + 1)
                def blocks(a, b):
                    return banks[6][:, a * E:b * E]

                for k in range(NT):
                    last = mm(blocks(k + 1, NT + 1).rearrange("p (k e) -> p k e", e=E), onesb[:],
                              ohb[:, k * E:(k + 1) * E].unsqueeze(1).broadcast_to([P, NT - k, E]),
                              start=(k == 0), stop=(k == NT - 1))
                    if k == 0:
                        mm(blocks(0, 1), trib[:], ohb[:, 0:E], start=False, stop=False)
                        mm(blocks(1, NT), trib[:], ohb[:, E:], start=False, stop=False)
                last.then_inc(s["rank_mm"], 1)
                pe.wait_ge(s["carried_ready"], layer + 1)
                pe.wait_ge(s["inv_in"], layer + 1)
                for k in range(NT):
                    last = mm(banks[4][:, 0:NV * SP2], ohr[:, k, :],
                              carried[:, k, :, :].rearrange("p v j -> p (v j)"),
                              start=(k == 0), stop=(k == NT - 1))
                last.then_inc(s["inv_done"], 1)
                pe.wait_ge(s["expert_ready"], layer + 1)

                def count(j):
                    return layer * SLOTS + j

                def step(i, u):
                    inner = not isinstance(i, int)
                    if has(i, 0):
                        pe.wait_ge(gathered[u], scatter_count(layer, i, u))
                        if inner or i >= 2:
                            pe.wait_ge(s["xT_evac"], count(i - 1))
                        nc.tensor.transpose(banks[u % 2][:, 0:P], xin[:, u, :], ident[:]) \
                            .then_inc(s["xT_mm"], 1)
                    if has(i, 1):
                        j, v = i - 1, (u - 1) % 2
                        pe.wait_ge(s["xT_evac"], count(j + 1))
                        pe.wait_ge(s["w1_staged"], count(j + 1))
                        if inner or j >= 2:
                            pe.wait_ge(s["h_ready"], count(j - 1))
                        for c in range(FC):
                            last = mm(banks[2 + v][:, c * P:(c + 1) * P], w1_slot[:, v, c * P:(c + 1) * P],
                                      xT[:, v, :], start=True, stop=True)
                        last.then_inc(s["h_mm"], 1)
                    if has(i, 2):
                        j, v = i - 2, u % 2
                        e = expert_of(j, mybir.EngineType.PE)
                        pe.wait_ge(s["h_ready"], count(j + 1))
                        if inner or j >= 2:
                            pe.wait_ge(s["y_ready"], count(j - 1))
                        for c in range(FC):
                            last = mm(banks[6 + v][:, 0:D], hh[:, v, c * P:(c + 1) * P],
                                      w2[:, ds(e * FF + c * P, P)], start=(c == 0), stop=(c == FC - 1))
                        last.then_inc(s["y_mm"], 1)

                slot_steps(pe, step, 2)

            layers(pe, one_layer)

        @block.vector
        def _(dve):
            v = nc.vector
            step = [0]

            def link(ins):
                ins.then_inc(s["dve_step"], 1)
                step[0] += 1
                dve.wait_ge(s["dve_step"], step[0])

            def tile_stats(t):
                return v.bn_stats(st[:, ds(t, 1), :].rearrange("p a k -> p (a k)"),
                                  xs[:, ds(t, 1), :].rearrange("p a d -> p (a d)")).then_inc(s["x_stats"], 1)

            def finish_stats(which):
                dve.wait_ge(s["x_stats"], which * NT)
                v.tensor_tensor(mean[:], st[:, :, 1], st[:, :, 4], ALU.add)
                v.tensor_tensor(half_gap[:], st[:, :, 1], st[:, :, 4], ALU.subtract)
                link(v.tensor_tensor(rstd[:], st[:, :, 2], st[:, :, 5], ALU.add))
                v.tensor_scalar(mean[:], mean[:], 0.5, None, ALU.mult)
                v.tensor_tensor(half_gap[:], half_gap[:], half_gap[:], ALU.mult)
                link(v.tensor_scalar(rstd[:], rstd[:], 1.0 / D, EPS, ALU.mult, ALU.add))
                v.scalar_tensor_tensor(rstd[:], half_gap[:], 0.25, rstd[:], ALU.mult, ALU.add) \
                    .then_inc(s["stats_ready"], 1)
                dve.wait_ge(s["rstd_ready"], which)

            def normalise_all():
                for t in range(NT):
                    normalise(cur[:, t, :], t).then_inc(s["ln_ready"], 1)

            def normalise(out, t):
                return v.tensor_scalar(out, xs[:, ds(t, 1), :].rearrange("p a d -> p (a d)"),
                                       mean[:, ds(t, 1)],
                                       rstd[:, ds(t, 1)], ALU.subtract, ALU.mult)

            dve.wait_ge(s["x_loaded"], 16)
            for t in range(NT):
                tile_stats(t)
            finish_stats(1)

            def make_masks():
                dve.wait_ge(s["w_loaded"], W_ATT)
                dve.wait_ge(s["consts_pool"], 4)
                v.tensor_scalar(mask_bias[0:S, :], mask_i[:], 0.0, MASKED, ALU.is_equal, ALU.mult)
                link(v.tensor_scalar(keep[:], mask_i[:], 0.0, None, ALU.not_equal))
                link(v.tensor_reduce(out=keep_any[:, 0:1], in_=keep[:], axis=AX, op=ALU.max))
                v.tensor_copy(keep_any[:, 1:P], keep_any[:, 0:1].broadcast_to([S, P - 1])) \
                    .then_inc(s["consts_dve"], 1)
                link(v.tensor_reduce(out=local[:], in_=head_of[:].rearrange("p (g j) -> p j g", j=4), axis=AX,
                                     op=ALU.add))
                link(v.tensor_copy(diag[:, 1, :, :], local[:].unsqueeze(2).broadcast_to([P, 4, S])))
                dve.wait_ge(s["consts_mm"], 1)
                v.tensor_tensor(diag[:, 0, :, :], banks[4][:, 0:S].unsqueeze(1).broadcast_to([P, 4, S]),
                                diag[:, 1, :, :], ALU.mult).then_inc(s["consts_dve"], 1)

            def xln_tile(t, u):
                if not isinstance(t, int) or t >= 2:
                    dve.wait_ge(s["tr_done"], t - 1)
                normalise(xln[:, u, :], t).then_inc(s["xln_ready"], 1)

            def values_evac(t, u):
                dve.wait_ge(s["proj_done"], t + 1)
                if not isinstance(t, int) or t >= 2:
                    dve.wait_ge(s["od_done"], 2 * (t - 1))
                v.tensor_tensor(vv[:, u, :].rearrange("p (b d) -> p b d", b=BT),
                                banks[7][:, 0:BT * D].rearrange("p (b d) -> p b d", b=BT),
                                bvr[:].unsqueeze(1).broadcast_to([P, BT, D]), ALU.add) \
                    .then_inc(s["v_evac"], 1)

            def scores_max(t, i, first):
                n = 4 * t + i
                dve.wait_ge(s["s_done"], n + 1)
                if not (first and i < 2):
                    dve.wait_ge(s["exp_done"], n - 1)
                v.tensor_reduce(out=nmax[:, i % 2, :], in_=banks[i % 2][:, :].rearrange("p (k t) -> p k t", k=4),
                                axis=AX, op=ALU.max, negate=True).then_inc(s["nmax_ready"], 1)

            def own_heads(t, u, b):
                m = 2 * t + b
                dve.wait_ge(s["od_done"], m + 1)
                if not isinstance(t, int) or m >= 1:
                    dve.wait_ge(s["od_summed"], m)
                v.tensor_tensor(od[:], banks[4][:, :], diag[:].rearrange("p w j s -> p (w j s)"), ALU.mult) \
                    .then_inc(s["od_read"], 1)
                dve.wait_ge(s["od_read"], m + 1)
                v.tensor_reduce(out=od_s[:, u, :, b, :], in_=od[:].rearrange("p (w j s) -> p w s j", w=2, j=4),
                                axis=AX, op=ALU.add).then_inc(s["od_summed"], 1)

            def attention_out(t, u):
                dve.wait_ge(s["od_summed"], 2 * t + 2)
                if not isinstance(t, int) or t >= 1:
                    dve.wait_ge(s["attn_ready"], t)
                v.reciprocal(rden[:], od_s[:, u, 1, :, :].rearrange("p b s -> p (b s)")) \
                    .then_inc(s["rden_ready"], 1)
                dve.wait_ge(s["rden_ready"], t + 1)
                v.tensor_tensor(attnT[:, u, :], od_s[:, u, 0, :, :].rearrange("p b s -> p (b s)"), rden[:],
                                ALU.mult).then_inc(s["attn_ready"], 1)

            def residual(t, u):
                xt = xs[:, ds(t, 1), :].rearrange("p a d -> p (a d)")
                v.tensor_tensor(xt, xt, bor[:], ALU.add).then_inc(s["xo_ready"], 1)
                dve.wait_ge(s["xo_ready"], t + 1)
                dve.wait_ge(s["wo_done"], t + 1)
                v.tensor_tensor(xt, banks[4][:, 0:D], xt, ALU.add).then_inc(s["x_updated"], 1)
                dve.wait_ge(s["x_updated"], t + 1)
                tile_stats(t)

            def tile(t, u, first, last):
                scores_max(t, 0, first)
                if not first:
                    own_heads(t - 1, 1 - u, 0)
                if not (isinstance(t, int) and t + 2 >= NT):
                    xln_tile(t + 2, u)
                scores_max(t, 1, first)
                if not first:
                    own_heads(t - 1, 1 - u, 1)
                scores_max(t, 2, first)
                if not first:
                    attention_out(t - 1, 1 - u)
                if not last:
                    values_evac(t + 1, 1 - u)
                scores_max(t, 3, first)
                if not first:
                    residual(t - 1, 1 - u)

            xln_tile(0, 0)
            xln_tile(1, 1)
            make_masks()
            values_evac(0, 0)
            pairs_of_tiles(dve, tile, None, None)
            own_heads(NT - 1, 1, 0)
            own_heads(NT - 1, 1, 1)
            attention_out(NT - 1, 1)
            residual(NT - 1, 1)
            dve.wait_ge(s["later_loaded"], W_LATER)
            link(v.tensor_tensor(bcr[:], bcr[:], bdr[:], ALU.add))

            finish_stats(2)
            normalise_all()
            for q in (1, 3):
                dve.wait_ge(s["t_done"], q + 1)
                v.tensor_copy(curT[:, q * 512:(q + 1) * 512], banks[q][:, :]).then_inc(s["t_evac"], 1)
            dve.wait_ge(s["scan_abs"], 1)
            link(v.tensor_scalar(sA[:], banks[4][:, :], bdl4[:, 0:1], 0.0, ALU.add, ALU.max))
            link(v.tensor_scalar(a_tmp[:, 3:4], a4[:], 0.0, None, ALU.max))
            dve.wait_ge(s["scan_soft"], 1)
            link(v.tensor_tensor(a4[:], a_tmp[:, 2:3], a_tmp[:, 3:4], ALU.add))
            link(v.tensor_tensor(sA[:], sA[:], sC[:], ALU.add))
            link(v.tensor_scalar(sB[:], sA[:], a4[:, 0:1], -1.0, ALU.mult, ALU.mult))
            link(v.tensor_tensor_scan(sD[:], not_first[:], sB[:], 0.0, ALU.mult, ALU.add))
            link(v.tensor_scalar(sD[:], sD[:], -20.0, 20.0, ALU.max, ALU.min))
            dve.wait_ge(s["scan_mm"], 2)
            link(v.scalar_tensor_tensor(sB[:], banks[5][:, :], bb4[:, 0:1], sA[:], ALU.add, ALU.mult))
            v.tensor_copy(a_tmp[:, 0:1], a_tmp[:, 0:1]).then_inc(s["scan_cum"], 1)
            dve.wait_ge(s["scan_exp"], 1)
            link(v.tensor_tensor(sB[:].rearrange("p (b t) -> p b t", t=S),
                                 sB[:].rearrange("p (b t) -> p b t", t=S), decay[:, :, 0:S], ALU.mult))
            link(v.tensor_tensor_scan(sC[:], not_first[:], sB[:], 0.0, ALU.mult, ALU.add))
            dve.wait_ge(s["scan_exp"], 2)
            v.tensor_tensor(sC[:], sC[:], sA[:], ALU.mult).then_inc(s["scan_h"], 1)
            dve.wait_ge(s["xb_ready"], 1)
            for q in range(4):
                dve.wait_ge(s["scan_out"], q + 1)
                xq = xs[:, 4 * q:4 * q + 4, :].rearrange("p t d -> p (t d)")
                v.tensor_tensor(xq, banks[q][:, :], xq, ALU.add).then_inc(s["x2_ready"], 1)
                dve.wait_ge(s["x2_ready"], q + 1)
                for t in range(4 * q, 4 * q + 4):
                    tile_stats(t)
            finish_stats(3)
            normalise_all()

            base_steps = step[0]
            CHAIN = 28

            def one_layer(layer, parity, two):
                done = [0]

                def chain(ins):
                    ins.then_inc(s["dve_step"], 1)
                    done[0] += 1
                    dve.wait_ge(s["dve_step"], layer * CHAIN + (base_steps + done[0]))

                def ke(ap):
                    return ap.rearrange("p (k e) -> p k e", e=E)

                def over_e(ap):
                    return ap.unsqueeze(2).broadcast_to([P, NT, E])

                def over_k(ap):
                    return ap.unsqueeze(1).broadcast_to([P, NT, E])

                v.tensor_copy(rnow[:, 0:E], rt[:, ds(layer, 1), :].rearrange("p a e -> p (a e)")) \
                    .then_inc(s["router_ready"], 1)
                for q in (1, 3):
                    dve.wait_ge(s["t_done"], layer * 4 + (4 + q + 1))
                    v.tensor_copy(curT[:, q * 512:(q + 1) * 512], banks[q][:, :]).then_inc(s["t_evac"], 1)
                dve.wait_ge(s["logits_done"], layer + 1)
                v.tensor_copy(lgT[:], banks[4][:, :]).then_inc(s["lgT_ready"], 1)
                dve.wait_ge(s["lg_done"], layer + 1)
                chain(v.tensor_copy(
                    lg[:].rearrange("p (j c e) -> p j c e", j=4, c=4),
                    banks[5][:, :].rearrange("p (c j e) -> p j c e", c=4, j=4)[:, :, :, 0:E]))
                chain(v.tensor_reduce(out=mx[:], in_=ke(lg[:]), axis=AX, op=ALU.max))
                v.tensor_tensor(ke(ex[:]), ke(lg[:]), over_e(mx[:]), ALU.subtract).then_inc(s["sh_ready"], 1)
                dve.wait_ge(s["ex_ready"], layer + 1)
                chain(v.tensor_reduce(out=sm[:], in_=ke(ex[:]), axis=AX, op=ALU.add))
                chain(v.reciprocal(sm[:], sm[:]))
                chain(v.tensor_tensor(ke(pr[:]), ke(ex[:]), over_e(sm[:]), ALU.mult))
                chain(v.tensor_reduce(out=wt[:], in_=ke(pr[:]), axis=AX, op=ALU.max))
                chain(v.tensor_tensor(ke(eq[:]), ke(pr[:]), over_e(wt[:]), ALU.is_equal))
                chain(v.tensor_tensor_scan(nth[:], not_first16[:], eq[:], 0.0, ALU.mult, ALU.add))
                v.scalar_tensor_tensor(ohb[:], nth[:], 1.0, eq[:], ALU.is_equal, ALU.mult) \
                    .then_inc(s["oh_ready"], 1)
                chain(v.tensor_copy(vals[:, :, 2], wt[:]))
                chain(v.tensor_tensor(wr[:], wt[:], vals[:, :, 2], ALU.subtract))
                chain(v.tensor_copy(vals[:, :, 3], wr[:]))
                v.tensor_tensor(vals[:, :, 4], wr[:], vals[:, :, 3], ALU.subtract)
                dve.wait_ge(s["rank_mm"], layer + 1)
                chain(v.tensor_tensor(ke(cmp[:]), banks[6][:, NT * E:(NT + 1) * E].unsqueeze(2)
                                      .broadcast_to([P, E, NT]), over_k(thr_gt[:]), ALU.is_gt))
                chain(v.tensor_reduce(out=nt[:], in_=ke(cmp[:]), axis=AX, op=ALU.add))
                chain(v.tensor_tensor_scan(itl[:], ones[:, 0:E], nt[:], 0.0, ALU.mult, ALU.add))
                chain(v.tensor_tensor(tb[:], itl[:], nt[:], ALU.subtract))
                chain(v.scalar_tensor_tensor(ke(rk[:]), over_k(tb[:]), float(P), ke(banks[6][:, 0:NT * E]),
                                             ALU.mult, ALU.add))
                chain(v.tensor_tensor(rk[:], rk[:], ohb[:], ALU.mult))
                chain(v.tensor_reduce(out=place[:], in_=ke(rk[:]), axis=AX, op=ALU.add))
                chain(v.tensor_copy(place_i[:], place[:]))
                v.tensor_scalar(row_i[:], place_i[:], P - 1, None, ALU.bitwise_and)
                chain(v.tensor_scalar(slot_i[:], place_i[:], P.bit_length() - 1, None, ALU.logical_shift_right))
                v.tensor_tensor(ohj[:], iota_j[:].unsqueeze(1).broadcast_to([P, NT, SP2]),
                                slot_i[:].unsqueeze(2).broadcast_to([P, NT, SP2]), ALU.is_equal) \
                    .then_inc(s["slots_hot"], 1)
                v.tensor_tensor(ohr[:], iota_r[:].unsqueeze(1).broadcast_to([P, NT, P]),
                                row_i[:].unsqueeze(2).broadcast_to([P, NT, P]), ALU.is_equal)
                dve.wait_ge(s["slots_hot"], layer + 1)
                v.tensor_tensor(carried[:, :, 0, :], ohj[:], vals[:, :, 0:1].broadcast_to([P, NT, SP2]),
                                ALU.mult).then_inc(s["inv_in"], 1)
                chain(v.tensor_tensor(scmp[:], iota_j[0:1, :].unsqueeze(2).broadcast_to([1, SP2, E]),
                                      itl[0:1, :].unsqueeze(1).broadcast_to([1, SP2, E]), ALU.is_ge))
                chain(v.tensor_reduce(out=sef[:], in_=scmp[:], axis=AX, op=ALU.add))
                v.tensor_scalar(slot_expert[:], sef[:], float(E - 1), None, ALU.min) \
                    .then_inc(s["expert_ready"], 1)
                dve.wait_ge(s["inv_done"], layer + 1)
                inv = banks[4][:, 0:NV * SP2].rearrange("p (v j) -> p v j", v=NV)
                chain(v.tensor_scalar(tok[:], inv[:, 1, :], float(P), None, ALU.mult))
                chain(v.tensor_tensor(tok[:], inv[:, 0, :], tok[:], ALU.add))
                v.tensor_scalar(gidx[:], tok[:], -1.0, 0.0, ALU.add, ALU.max).then_inc(s["gidx_ready"], 1)
                chain(v.scalar_tensor_tensor(pad[:], inv[:, 0, :], 0.0, dump_row[:], ALU.is_equal, ALU.mult))
                v.scalar_tensor_tensor(sidx[:], tok[:], -1.0, pad[:], ALU.add, ALU.add)
                chain(v.tensor_copy(wslot[:], inv[:, 2, :]))
                chain(v.tensor_tensor(wslot[:], inv[:, 3, :], wslot[:], ALU.add))
                chain(v.tensor_tensor(wslot[:], inv[:, 4, :], wslot[:], ALU.add))
                assert done[0] == CHAIN, done

                def count(j):
                    return layer * SLOTS + j

                def step(i, u):
                    inner = not isinstance(i, int)
                    if has(i, 1):
                        j, p2 = i - 1, (u - 1) % 2
                        dve.wait_ge(s["tanh_done"], count(j + 1))
                        if inner or j >= 2:
                            dve.wait_ge(s["y_mm"], count(j - 1))
                        v.scalar_tensor_tensor(hh[:, p2, :], th[:, p2, :], 1.0, banks[2 + p2][:, :],
                                               ALU.add, ALU.mult).then_inc(s["h_ready"], 1)
                    if has(i, 2):
                        j, p2, p4 = i - 2, u % 2, (u - 2) % 4
                        dve.wait_ge(s["y_mm"], count(j + 1))
                        if inner or j >= 4:
                            dve.wait_ge(scattered[p4], scatter_count(layer, j - 4, p4))
                        v.tensor_scalar(yout[:, p4, :], banks[6 + p2][:, 0:D], wslot[:, ds(j, 1)], 0.5,
                                        ALU.mult, ALU.mult).then_inc(s["y_ready"], 1)

                slot_steps(dve, step, 2)

            layers(dve, one_layer)
            for q in range(4):
                dve.wait_ge(cur_loaded[q], (L + 1) * 16)
                xq = xs[:, 4 * q:4 * q + 4, :]
                v.tensor_tensor(xq, xq, cur[:, 4 * q:4 * q + 4, :], ALU.add).then_inc(s["out_ready"], 1)


_INS = ['x', 'ctx_1024', 'mask_SxS2_ik0', 'L0_xattn_Wq', 'L0_xattn_bq', 'L0_xattn_Wk', 'L0_xattn_bk',
        'L0_xattn_Wv', 'L0_xattn_bv', 'L0_xattn_Wo', 'L0_xattn_bo', 'L0_attn_A', 'L0_attn_Wb',
        'L0_attn_bb', 'L0_attn_Wc', 'L0_attn_bc', 'L0_attn_Wd', 'L0_attn_bd', 'L0_attn_Wdelta',
        'L0_attn_bdelta', 'L0_ffn_routers', 'L0_ffn_W1', 'L0_ffn_W2']


def kernel(**inputs):
    import numpy as _np
    import concourse.bacc as _bacc
    from concourse import mybir as _mybir
    from concourse.bass_utils import run_bass_kernel_spmd as _run

    nc = _bacc.Bacc("TRN2", target_bir_lowering=False, num_devices=1)
    arrays, args = {}, []
    for name in _INS:
        a = _np.ascontiguousarray(inputs[name])
        arrays[f"in_{name}_dram"] = a
        args.append(nc.dram_tensor(f"in_{name}_dram", a.shape, _mybir.dt.from_np(a.dtype), kind="ExternalInput").ap())
    shape = inputs["x"].shape
    args.append(nc.dram_tensor("out_0_dram", shape, _mybir.dt.from_np(_np.dtype("float32")), kind="ExternalOutput").ap())
    perceiver_block(nc, *args)
    r = _run(nc, [arrays], core_ids=[0])
    return r.results[0]["out_0_dram"]
```

```python
from contextlib import ExitStack

import concourse.bass as bass
from concourse import mybir

P = 128
F32 = mybir.dt.float32
BF16 = mybir.dt.bfloat16
I32 = mybir.dt.int32
ACT = mybir.ActivationFunctionType
ALU = mybir.AluOpType
AX = mybir.AxisListType.X

EPS = 1e-5
MASKED = -1e30
HEADS = 16


def ds(start, size):
    return bass.ds(start, size)


def perceiver_block(nc, x, ctx, mask, Wq, bq, Wk, bk, Wv, bv, Wo, bo, A, Wb, bb, Wc, bc, Wd, bd,
                    Wdelta, bdelta, routers, W1, W2, out):
    B, S, D = x.shape
    T = ctx.shape[1]
    HD = D // HEADS
    H = A.shape[0]
    L, _, E = routers.shape
    FF = W1.shape[2]
    N = B * S
    NT = N // P
    BT = P // S
    NG = P // H
    GT = NT // NG
    GW = GT * P
    PIECES = NT + E - 1
    PC = 32
    FC = FF // P
    FIRST = 4
    PAIRS = HEADS // 2
    NV = 5
    assert D == P and T == P and S * 2 == P and NG == 4 and E == 16 and L % 2 == 0

    x_t = x.rearrange("b s d -> (b s) d").rearrange("(t p) d -> p t d", p=P)
    out_t = out.rearrange("b s d -> (b s) d").rearrange("(t p) d -> p t d", p=P)
    ctx_t = ctx.rearrange("b t d -> t b d")
    rows = [nc.dram_tensor(f"token_rows_{i}", (N, D), F32, kind="Internal").ap() for i in range(2)]

    def col(v):
        return v.rearrange("(n a) -> n a", a=1)

    with ExitStack() as stack:
        def sb(name, shape, dt=F32):
            return stack.enter_context(nc.sbuf_tensor(name, shape, dt))

        def sem(name):
            return stack.enter_context(nc.semaphore(name))

        banks = [stack.enter_context(nc.psum_tensor(f"bank{i}", [P, 512], F32)) for i in range(8)]

        wq, wk, wv, wo, wd = (sb(n, [P, D]) for n in ("wq", "wk", "wv", "wo", "wd"))
        wdl, wb = sb("wdl", [D, H]), sb("wb", [D, H])
        wc_own = sb("wc_own", [P, NG, D])
        w1 = sb("w1", [P, E * FF])
        w2 = sb("w2", [P, E * FF])
        rt = sb("rt", [P, L, E])
        rnow = sb("rnow", [P, 32])
        bqc, bkc = sb("bqc", [P, 1]), sb("bkc", [P, 1])
        bvr, bor, bcr, bdr = (sb(n, [P, D]) for n in ("bvr", "bor", "bcr", "bdr"))
        bdl4, bb4, a4 = sb("bdl4", [P, 1]), sb("bb4", [P, 1]), sb("a4", [P, 1])
        a_tmp = sb("a_tmp", [P, 4])
        ident = sb("ident", [P, P])
        ones = sb("ones", [P, P])
        onesb = sb("onesb", [P, P], BF16)
        trib = sb("trib", [P, P], BF16)
        pair_rows = sb("pair_rows", [P, P], BF16)
        mask_i = sb("mask_i", [S, T], I32)
        mask_bias = sb("mask_bias", [P, T], BF16)
        keep = sb("keep", [S, T])
        keep_any = sb("keep_any", [S, P])
        head_of = sb("head_of", [P, HEADS])
        local = sb("local", [P, 4])
        diag = sb("diag", [P, 2, 4, S])
        iota_r = sb("iota_r", [P, P])
        iota_j = sb("iota_j", [P, PC])
        iota_e1 = sb("iota_e1", [1, E])
        sorted_pos = sb("sorted_pos", [P, NT])
        not_first = sb("not_first", [P, GW])
        not_first16 = sb("not_first16", [P, 256])
        vals = sb("vals", [P, NT, NV], BF16)
        xs = sb("xs", [P, NT, D])
        cur = sb("cur", [P, NT, D])
        curT = sb("curT", [P, N])
        st = sb("st", [P, NT, 6])
        mean = sb("mean", [P, NT])
        half_gap = sb("half_gap", [P, NT])
        rstd = sb("rstd", [P, NT])
        offset = sb("offset", [P, NT])
        xln = sb("xln", [P, 2, D])
        cx = sb("cx", [P, 2, BT, D])
        aT = sb("aT", [P, 2, 3 * P])
        qT = sb("qT", [P, 2, P])
        qm = sb("qm", [P, 2, BT * HEADS * S])
        kT = sb("kT", [P, 2, BT * T])
        vv = sb("vv", [P, 2, BT * D])
        nmax = sb("nmax", [P, 2, 4])
        pp = sb("pp", [P, 2, 512])
        ppT = sb("ppT", [P, 4, 512])
        od = sb("od", [P, 512])
        od_s = sb("od_s", [P, 2, 2, BT, S])
        rden = sb("rden", [P, BT * S])
        attnT = sb("attnT", [P, 2, P])
        sA, sB, sC, sD = (sb(n, [P, GW]) for n in ("sA", "sB", "sC", "sD"))
        decay = sb("decay", [P, GW // S, S + 1])
        lgT = sb("lgT", [P, 512])
        ex, eq, nth, rk = (sb(n, [P, 256]) for n in ("ex", "eq", "nth", "rk"))
        ohb = sb("ohb", [P, 256], BF16)
        mx, sm, wt, ends, starts, place, wr = (sb(n, [P, 16]) for n in
                                               ("mx", "sm", "wt", "ends", "starts", "place", "wr"))
        place_i, row_i, tile_i = (sb(n, [P, NT], I32) for n in ("place_i", "row_i", "tile_i"))
        ohr = sb("ohr", [P, NT, P], BF16)
        oht = sb("oht", [P, NT, NT], BF16)
        carried = sb("carried", [P, NT, NV, NT], BF16)
        token_i = sb("token_i", [P, NT], I32)
        token, expert_at, piece_at, wsort = (sb(n, [P, NT]) for n in ("token", "expert_at", "piece_at", "wsort"))
        ends_cmp = sb("ends_cmp", [P, NT, E])
        piece_hot = sb("piece_hot", [P, PC, NT])
        wpiece = sb("wpiece", [P, PC])
        end_i = sb("end_i", [1, E], I32)
        first_piece = sb("first_piece", [1, E])
        pcmp = sb("pcmp", [1, PC, E - 1])
        pexp, pexp_tile = sb("pexp", [1, PC]), sb("pexp_tile", [1, PC])
        piece_expert = sb("piece_expert", [1, PC], I32)
        piece_tile = sb("piece_tile", [1, PC], I32)
        xin = qm[:, 0, 0:4 * D].rearrange("p (u d) -> p u d", u=4)
        xT = qm[:, 1, :]
        ysort = sb("ysort", [P, NT, D])
        th = sb("th", [P, 2, FF])
        hh = sb("hh", [P, 2, FF])
        w1_piece = sb("w1_piece", [P, 2, FF])

        names = """x_first_loaded x_loaded w_loaded later_loaded w1_loaded w2_loaded stored rows_stored
            consts_pool consts_dve consts_mm dve_step act_step
            stats_ready sqrt_ready offset_ready ln_even ln_odd
            xln_ready tr_done a_evac proj_done q_evac k_evac v_evac qm_ready s_done exp_done
            pt_done pt_evac od_done od_read attn_ready wo_done x_updated x_stats xb_ready
            t_done t_evac scan_mm scan_abs scan_soft scan_cum scan_b scan_exp scan_h scan_out x2_ready
            router_ready logits_done lgT_ready lg_done sh_ready ex_ready oh_ready rank_mm
            tiles_hot carried_ready inv_in inv_done tokens_ready pieces_ready y_zeroed
            nmax_ready od_summed rden_ready xo_ready
            waited_alone xT_mm xT_evac w1_staged h_mm tanh_done h_ready y_mm y_ready
            out_ready""".split()
        s = dict(zip(names, [sem(n) for n in names]))
        ctx_loaded = [sem(f"ctx_loaded{u}") for u in range(2)]
        gathered = [sem(f"gathered{u}") for u in range(4)]
        scattered = [sem(f"scattered{u}") for u in range(4)]
        cur_loaded = [sem(f"cur_loaded{q}") for q in range(4)]
        OF_FOUR = 16 * NT // 4

        attention_weights = [
            (wk[:], Wk), (wv[:], Wv), (wq[:], Wq), (mask_i[:], mask), (bqc[:], col(bq)), (bkc[:], col(bk)),
            (bvr[:], bv.partition_broadcast(P)), (wo[:], Wo), (bor[:], bo.partition_broadcast(P))]
        later_weights = [
            (wdl[:], Wdelta), (wb[:], Wb), (wd[:], Wd), (rt[:], routers.rearrange("l d e -> d l e")),
            (bcr[:], bc.partition_broadcast(P)), (bdr[:], bd.partition_broadcast(P))]
        later_weights += [(dst[g * H:(g + 1) * H, :], src) for g in range(NG)
                          for dst, src in ((wc_own[:, g, :], Wc), (bdl4, col(bdelta)), (bb4, col(bb)),
                                           (a4, col(A)))]
        W_ATT = 16 * len(attention_weights)
        W_LATER = 16 * len(later_weights)

        def pairs_of_tiles(eng, body, first, last):
            body(0, 0, first=True, last=False)
            body(1, 1, first=False, last=False)
            with eng.Fori(2, NT - 3, 2) as t:
                body(t, 0, first=False, last=False)
                body(t + 1, 1, first=False, last=False)
            body(NT - 2, 0, first=False, last=False)
            body(NT - 1, 1, first=False, last=True)

        def layers(eng, body):
            with eng.Fori(0, L // 2) as two:
                for parity in range(2):
                    body(two * 2 + parity, parity, two)

        def piece_steps(step):
            for i in range(PIECES + 2):
                step(i)

        def entry(table, piece, engine, most):
            return nc.values_load(
                table[0:1, piece:piece + 1], engines=[engine], min_val=0, max_val=most,
                skip_runtime_bounds_check_because="the vector engine computes it within these bounds")

        def wait_alone(eng, which, value):
            eng.wait_ge(which, value)
            eng.sem_inc(s["waited_alone"], 1)

        def wait_normalised(eng, nth, q):
            eng.wait_ge(s["ln_even"] if q % 2 == 0 else s["ln_odd"], 2 * nth + (q // 2 + 1))

        block = stack.enter_context(nc.Block())

        @block.sync
        def _(sp):
            sp.dma_start(xs[:, 0:FIRST, :], x_t[:, 0:FIRST, :]).then_inc(s["x_first_loaded"], 16)
            def load_ctx(t, u, first, last):
                if not isinstance(t, int) or t >= 2:
                    wait_alone(sp, s["tr_done"], t - 1)
                sp.dma_start(cx[:, u, :, :], ctx_t[:, ds(t * BT, BT), :]).then_inc(ctx_loaded[u], 16)

            load_ctx(0, 0, True, False)
            for dst, src in attention_weights:
                sp.dma_start(dst, src).then_inc(s["w_loaded"], 16)
            load_ctx(1, 1, True, False)
            sp.dma_start(xs[:, FIRST:NT, :], x_t[:, FIRST:NT, :]).then_inc(s["x_loaded"], 16)
            sp.wait_ge(s["consts_pool"], 1)
            for dst, src in later_weights:
                sp.dma_start(dst, src).then_inc(s["later_loaded"], 16)
            with sp.Fori(2, NT - 1, 2) as t:
                load_ctx(t, 0, False, False)
                load_ctx(t + 1, 1, False, False)
            sp.dma_start(w1[:].rearrange("p (e f) -> p e f", e=E), W1.rearrange("e d f -> d e f")) \
                .then_inc(s["w1_loaded"], 16)
            sp.dma_start(w2[:].rearrange("p (e c d) -> p e c d", e=E, c=FC),
                         W2.rearrange("e (c p) d -> p e c d", p=P)).then_inc(s["w2_loaded"], 16)
            for q in range(4):
                wait_normalised(sp, 1, q)
                sp.sem_inc(cur_loaded[q], 16)
            sp.dma_start(rows[0][0:N, :].rearrange("(t p) d -> p t d", p=P), cur[:]) \
                .then_inc(s["rows_stored"], 16)

            def load_next(layer, source):
                wait_alone(sp, s["t_done"], (layer + 2) * 4)
                for u in range(4):
                    wait_alone(sp, scattered[u], (layer + 1) * OF_FOUR)
                for q in range(4):
                    sp.dma_start(cur[:, 4 * q:4 * q + 4, :],
                                 source[q * 4 * P:(q + 1) * 4 * P, :].rearrange("(t p) d -> p t d", p=P)) \
                        .then_inc(cur_loaded[q], 16)

            with sp.Fori(0, L // 2) as two:
                load_next(two * 2, rows[1])
                load_next(two * 2 + 1, rows[0])
            for q in range(4):
                sp.wait_ge(s["out_ready"], q + 1)
                sp.dma_start(out_t[:, 4 * q:4 * q + 4, :], xs[:, 4 * q:4 * q + 4, :]).then_inc(s["stored"], 16)
            sp.wait_ge(s["rows_stored"], 16)
            sp.wait_ge(s["stored"], 64)

        @block.gpsimd
        def _(pool):
            g = nc.gpsimd
            g.memset(ident[:], 0.0)
            g.memset(ones[:], 1.0)
            g.memset(onesb[:], 1.0)
            g.memset(head_of[:], 1.0)
            g.memset(mask_bias[:], 0.0)
            g.memset(rnow[:], 0.0)
            g.memset(wc_own[:], 0.0)
            g.memset(not_first[:], 1.0)
            g.memset(not_first16[:], 1.0)
            g.memset(decay[:], 1.0).then_inc(s["consts_pool"], 1)
            for dst, pat, base, cm in [
                    (iota_r[:], [[1, P]], 0, 0),
                    (iota_j[:], [[1, PC]], 0, 0), (iota_e1[:], [[1, E]], 1, 0),
                    (sorted_pos[:], [[P, NT]], 0, 1),
                    (vals[:, :, 0], [[0, NT]], 0, 1), (vals[:, :, 1], [[P, NT]], 0, 0)]:
                last = g.iota(dst, pattern=pat, base=base, channel_multiplier=cm,
                              allow_small_or_imprecise_dtypes=True)
            last.then_inc(s["consts_pool"], 1)
            pool.wait_ge(s["consts_pool"], 2)
            g.affine_select(out=ident[:], in_=ident[:], compare_op=ALU.not_equal, fill=1.0, base=0,
                            pattern=[[-1, P]], channel_multiplier=1)
            g.affine_select(out=trib[:], in_=onesb[:], compare_op=ALU.is_gt, fill=0.0, base=0,
                            pattern=[[1, P]], channel_multiplier=-1)
            g.affine_select(out=head_of[:], in_=head_of[:], compare_op=ALU.is_ge, fill=0.0, base=0,
                            pattern=[[-HD, HEADS]], channel_multiplier=1).then_inc(s["consts_pool"], 1)
            pool.wait_ge(s["consts_pool"], 3)
            g.affine_select(out=head_of[:], in_=head_of[:], compare_op=ALU.is_ge, fill=0.0, base=HD - 1,
                            pattern=[[HD, HEADS]], channel_multiplier=-1)
            nf = not_first[:].rearrange("p (b t) -> p b t", t=S)
            g.memset(nf[:, :, 0:1], 0.0)
            nf16 = not_first16[:].rearrange("p (e k) -> p e k", k=NT)
            g.memset(nf16[:, :, 0:1], 0.0)
            g.tensor_copy(pair_rows[:, 0:S], ident[:, 0:S])
            g.tensor_copy(pair_rows[:, S:P], ident[:, 0:S]).then_inc(s["consts_pool"], 1)

            def masked_queries(t, u, first, last):
                pool.wait_ge(s["q_evac"], t + 1)
                if not isinstance(t, int) or t >= 2:
                    pool.wait_ge(s["s_done"], 4 * (t - 1))
                for b in range(BT):
                    w = HEADS * S
                    g.tensor_tensor(
                        qm[:, u, b * w:(b + 1) * w].rearrange("p (h s) -> p h s", h=HEADS),
                        qT[:, u, b * S:(b + 1) * S].unsqueeze(1).broadcast_to([P, HEADS, S]),
                        head_of[:].unsqueeze(2).broadcast_to([P, HEADS, S]), ALU.mult) \
                        .then_inc(s["qm_ready"], 1)

            pairs_of_tiles(pool, masked_queries, None, None)
            wait_normalised(pool, 0, 2)
            wait_normalised(pool, 0, 3)
            g.tensor_tensor(xs[:], xs[:], bcr[:].unsqueeze(1).broadcast_to([P, NT, D]), ALU.add) \
                .then_inc(s["xb_ready"], 1)

            pool.wait_ge(s["rows_stored"], 16)

            g.memset(ysort[:], 0.0).then_inc(s["y_zeroed"], 1)

            def one_layer(layer, parity, two):
                src, dst = rows[parity], rows[1 - parity]
                wait_alone(pool, s["tiles_hot"], layer + 1)
                for n in range(2, NV):
                    last = g.tensor_tensor(carried[:, :, n, :], oht[:],
                                           vals[:, :, n:n + 1].broadcast_to([P, NT, NT]), ALU.mult)
                last.then_inc(s["carried_ready"], 1)
                wait_alone(pool, s["tokens_ready"], layer + 1)
                for i in range(NT):
                    if i >= 4:
                        wait_alone(pool, s["xT_mm"], layer * NT + (i - 3))
                    g.indirect_dma_start(
                        out=xin[:, i % 4, :], out_offset=None, in_=src,
                        in_offset=bass.IndirectOffsetOnAxis(ap=token_i[:, i:i + 1], axis=0)) \
                        .then_inc(gathered[i % 4], 16)
                for i in range(NT):
                    wait_alone(pool, s["y_ready"], layer * PIECES + (i + E))
                    g.indirect_dma_start(
                        out=dst, out_offset=bass.IndirectOffsetOnAxis(ap=token_i[:, i:i + 1], axis=0),
                        in_=ysort[:, i, :], in_offset=None).then_inc(scattered[i % 4], 16)
                for u in range(4):
                    wait_alone(pool, scattered[u], (layer + 1) * OF_FOUR)
                g.memset(ysort[:], 0.0).then_inc(s["y_zeroed"], 1)

            layers(pool, one_layer)

        @block.scalar
        def _(act):
            a = nc.scalar
            def std_of(n, tiles):
                act.wait_ge(s["stats_ready"], n)
                a.activation(rstd[:, tiles], rstd[:, tiles], ACT.Sqrt).then_inc(s["sqrt_ready"], 1)

            def normalise_odd_quarters(nth):
                act.wait_ge(s["offset_ready"], nth + 1)
                for q in (1, 3):
                    for t in range(4 * q, 4 * q + 4):
                        last = a.activation(cur[:, t, :], xs[:, t, :], ACT.Identity, bias=offset[:, t:t + 1],
                                            scale=rstd[:, t:t + 1])
                    last.then_inc(s["ln_odd"], 1)

            step = [0]
            std_of(1, slice(0, FIRST))
            act.wait_ge(s["w_loaded"], W_ATT)
            a.mul(bqc[:], bqc[:], float(HD) ** -0.5).then_inc(s["act_step"], 1)
            step[0] += 1
            act.wait_ge(s["act_step"], step[0])

            def evac_inputs(t, u):
                act.wait_ge(s["tr_done"], t + 1)
                if not isinstance(t, int) or t >= 2:
                    act.wait_ge(s["proj_done"], t - 1)
                a.copy(aT[:, u, :], banks[5][:, 0:3 * P]).then_inc(s["a_evac"], 1)

            def evac_qk(t, u):
                act.wait_ge(s["proj_done"], t + 1)
                if not isinstance(t, int) or t >= 2:
                    act.wait_ge(s["qm_ready"], 2 * (t - 1))
                    act.wait_ge(s["s_done"], 4 * (t - 1))
                a.activation(qT[:, u, :], banks[6][:, 0:P], ACT.Identity, bias=bqc[:, 0:1],
                             scale=float(HD) ** -0.5).then_inc(s["q_evac"], 1)
                a.activation(kT[:, u, :], banks[6][:, P:3 * P], ACT.Identity, bias=bkc[:, 0:1],
                             scale=1.0).then_inc(s["k_evac"], 1)

            def exp_scores(t, i, first):
                n = 4 * t + i
                act.wait_ge(s["nmax_ready"], n + 1)
                if not (first and i < 2):
                    act.wait_ge(s["pt_done"], n - 1)
                for k in range(4):
                    last = a.activation(pp[:, i % 2, k * T:(k + 1) * T], banks[i % 2][:, k * T:(k + 1) * T],
                                        ACT.Exp, bias=nmax[:, i % 2, k:k + 1], scale=1.0)
                last.then_inc(s["exp_done"], 1)

            def evac_pt(t, i):
                n = 4 * t + i
                act.wait_ge(s["pt_done"], n + 1)
                if not isinstance(t, int) or t >= 1:
                    act.wait_ge(s["od_done"], 2 * t + (i // 2 - 1))
                a.copy(ppT[:, i, :], banks[2 + i % 2][:, :]).then_inc(s["pt_evac"], 1)

            def tile(t, u, first, last):
                if not first:
                    evac_pt(t - 1, 2)
                exp_scores(t, 0, first)
                if not first:
                    evac_pt(t - 1, 3)
                if not last:
                    evac_qk(t + 1, 1 - u)
                exp_scores(t, 1, first)
                evac_pt(t, 0)
                if not (isinstance(t, int) and t + 2 >= NT):
                    evac_inputs(t + 2, u)
                exp_scores(t, 2, first)
                evac_pt(t, 1)
                exp_scores(t, 3, first)

            evac_inputs(0, 0)
            evac_inputs(1, 1)
            evac_qk(0, 0)
            std_of(2, slice(FIRST, NT))
            pairs_of_tiles(act, tile, None, None)
            evac_pt(NT - 1, 2)
            evac_pt(NT - 1, 3)

            def evac_tiles():
                for q in (1, 3):
                    act.wait_ge(s["t_done"], q + 1)
                    a.copy(curT[:, q * 512:(q + 1) * 512], banks[q][:, :]).then_inc(s["t_evac"], 1)

            std_of(3, slice(0, NT))
            normalise_odd_quarters(0)
            evac_tiles()
            act.wait_ge(s["later_loaded"], W_LATER)
            a.activation(a_tmp[:, 0:1], a4[:], ACT.Abs).then_inc(s["act_step"], 1)
            step[0] += 1
            act.wait_ge(s["act_step"], step[0])
            a.activation(a_tmp[:, 1:2], a_tmp[:, 0:1], ACT.Exp, scale=-1.0)
            act.wait_ge(s["scan_mm"], 1)
            a.activation(sC[:], banks[4][:, :], ACT.Abs, bias=bdl4[:, 0:1]).then_inc(s["scan_abs"], 1)
            act.wait_ge(s["scan_abs"], 1)
            a.activation(sC[:], sC[:], ACT.Exp, scale=-1.0).then_inc(s["act_step"], 1)
            step[0] += 1
            act.wait_ge(s["act_step"], step[0])
            a.activation(sC[:], sC[:], ACT.Ln, bias=1.0)
            a.activation(a_tmp[:, 2:3], a_tmp[:, 1:2], ACT.Ln, bias=1.0).then_inc(s["scan_soft"], 1)
            act.wait_ge(s["scan_cum"], 1)
            a.activation(decay[:, :, 1:S + 1], sD[:].rearrange("p (b t) -> p b t", t=S), ACT.Exp,
                         scale=-1.0).then_inc(s["scan_exp"], 1)
            act.wait_ge(s["scan_b"], 1)
            a.activation(sA[:], sD[:], ACT.Exp).then_inc(s["scan_exp"], 1)
            std_of(4, slice(0, NT))
            normalise_odd_quarters(1)

            def one_layer(layer, parity, two):
                done = layer * 4 + 4
                for q in (0, 2):
                    act.wait_ge(s["t_done"], done + (q + 1))
                    a.copy(curT[:, q * 512:(q + 1) * 512], banks[q][:, :]).then_inc(s["t_evac"], 1)
                act.wait_ge(s["sh_ready"], layer + 1)
                a.activation(ex[:], ex[:], ACT.Exp).then_inc(s["ex_ready"], 1)

                wait_alone(act, s["pieces_ready"], layer + 1)

                def step(i):
                    if i < PIECES:
                        e = entry(piece_expert, i, mybir.EngineType.Activation, E - 1)
                        if i >= 2:
                            act.wait_ge(s["h_mm"], layer * PIECES + (i - 1))
                        a.copy(w1_piece[:, i % 2, :], w1[:, ds(e * FF, FF)]).then_inc(s["w1_staged"], 1)
                    if i < NT:
                        act.wait_ge(s["xT_mm"], layer * NT + (i + 1))
                        a.copy(xT[:, i * P:(i + 1) * P], banks[i % 2][:, 0:P]).then_inc(s["xT_evac"], 1)
                    if 0 <= i - 1 < PIECES:
                        j = i - 1
                        act.wait_ge(s["h_mm"], layer * PIECES + (j + 1))
                        if j >= 2:
                            act.wait_ge(s["h_ready"], layer * PIECES + (j - 1))
                        a.activation(th[:, j % 2, :], banks[2 + j % 2][:, :], ACT.Tanh, scale=0.5) \
                            .then_inc(s["tanh_done"], 1)

                piece_steps(step)

            layers(act, one_layer)

        @block.tensor
        def _(pe):
            mm = nc.tensor.matmul
            pe.wait_ge(s["consts_pool"], 4)

            def transposes_in(t, u):
                pe.wait_ge(s["xln_ready"], t + 1)
                pe.wait_ge(ctx_loaded[u], (t - u) * 8 + 16)
                if not isinstance(t, int) or t >= 1:
                    pe.wait_ge(s["a_evac"], t)
                nc.tensor.transpose(banks[5][:, 0:P], xln[:, u, :], ident[:])
                nc.tensor.transpose(banks[5][:, P:2 * P], cx[:, u, 0, :], ident[:])
                nc.tensor.transpose(banks[5][:, 2 * P:3 * P], cx[:, u, 1, :], ident[:]) \
                    .then_inc(s["tr_done"], 1)

            def project(t, u):
                pe.wait_ge(s["a_evac"], t + 1)
                if not isinstance(t, int) or t >= 1:
                    pe.wait_ge(s["k_evac"], t)
                    pe.wait_ge(s["v_evac"], t)
                for b in range(BT):
                    mm(banks[7][:, b * D:(b + 1) * D], aT[:, u, (1 + b) * P:(2 + b) * P], wv[:],
                       start=True, stop=True)
                mm(banks[6][:, 0:P], wq[:], aT[:, u, 0:P], start=True, stop=True)
                mm(banks[6][:, P:3 * P], wk[:], aT[:, u, P:3 * P], start=True, stop=True) \
                    .then_inc(s["proj_done"], 1)

            def scores(t, u, i, first):
                n = 4 * t + i
                b, half = i // 2, i % 2
                if half == 0:
                    pe.wait_ge(s["qm_ready"], 2 * t + (b + 1))
                if i == 0:
                    pe.wait_ge(s["k_evac"], t + 1)
                if not (first and i < 2):
                    pe.wait_ge(s["exp_done"], n - 1)
                bank = banks[i % 2]
                mm(bank[:, :].rearrange("p (k t) -> p k t", k=4), pair_rows[:],
                   mask_bias[:].unsqueeze(1).broadcast_to([P, 4, T]), start=True, stop=False)
                for k in range(4):
                    c = ((b * HEADS) + (half * 4 + k) * 2) * S
                    last = mm(bank[:, k * T:(k + 1) * T], qm[:, u, c:c + P], kT[:, u, b * T:(b + 1) * T],
                              start=False, stop=(k == 3))
                last.then_inc(s["s_done"], 1)

            def transpose_probs(n, i4, early):
                pe.wait_ge(s["exp_done"], n + 1)
                if not early:
                    pe.wait_ge(s["pt_evac"], n - 1)
                for k in range(4):
                    last = nc.tensor.transpose(banks[2 + i4 % 2][:, k * P:(k + 1) * P],
                                               pp[:, i4 % 2, k * P:(k + 1) * P], ident[:])
                last.then_inc(s["pt_done"], 1)

            def values(t, u, b, early):
                pe.wait_ge(s["pt_evac"], 4 * t + 2 * b + 2)
                if b == 0:
                    pe.wait_ge(s["v_evac"], t + 1)
                if not early:
                    if b == 0:
                        pe.wait_ge(s["x_updated"], t)
                    else:
                        pe.wait_ge(s["od_read"], 2 * t + 1)
                for which in range(2):
                    for g in range(4):
                        lhsT = vv[:, u, b * D + 32 * g:b * D + 32 * g + 32] if which == 0 else ones[:, 0:32]
                        src = ppT[:, 2 * b + g // 2, (g % 2) * 256:(g % 2) * 256 + 256]
                        last = mm(banks[4][32 * g:32 * g + 32, which * 256:(which + 1) * 256], lhsT, src,
                                  start=True, stop=True)
                last.then_inc(s["od_done"], 1)

            def project_out(t, u):
                pe.wait_ge(s["attn_ready"], t + 1)
                mm(banks[4][:, 0:D], attnT[:, u, :], wo[:], start=True, stop=True).then_inc(s["wo_done"], 1)

            def tile(t, u, first, last):
                n = 4 * t
                again = isinstance(t, int) and t == 1
                scores(t, u, 0, first)
                if not first:
                    transpose_probs(n - 2, 2, False)
                    values(t - 1, 1 - u, 0, again)
                if not last:
                    project(t + 1, 1 - u)
                if not first:
                    transpose_probs(n - 1, 3, False)
                scores(t, u, 1, first)
                if not first:
                    values(t - 1, 1 - u, 1, False)
                scores(t, u, 2, False)
                transpose_probs(n, 0, first)
                if not (isinstance(t, int) and t + 2 >= NT):
                    transposes_in(t + 2, u)
                scores(t, u, 3, False)
                transpose_probs(n + 1, 1, first)
                if not first:
                    project_out(t - 1, 1 - u)

            transposes_in(0, 0)
            transposes_in(1, 1)
            pe.wait_ge(s["w_loaded"], W_ATT)
            project(0, 0)
            pe.wait_ge(s["consts_dve"], 1)
            mm(banks[4][:, 0:S], keep_any[:, :], ident[0:S, 0:S], start=True, stop=True) \
                .then_inc(s["consts_mm"], 1)
            pe.wait_ge(s["consts_dve"], 2)
            pairs_of_tiles(pe, tile, None, None)
            transpose_probs(4 * NT - 2, 2, False)
            values(NT - 1, 1, 0, False)
            transpose_probs(4 * NT - 1, 3, False)
            values(NT - 1, 1, 1, False)
            project_out(NT - 1, 1)

            def stay_warm(bank, products):
                for n in range(products):
                    mm(bank[:, :].rearrange("p (k t) -> p k t", k=4), onesb[:],
                       trib[:].unsqueeze(1).broadcast_to([P, 4, P]), start=True, stop=True)

            def transpose_tiles(wait_for_quarter):
                for q in range(4):
                    wait_for_quarter(q)
                    for k in range(4):
                        last = nc.tensor.transpose(banks[q][:, k * P:(k + 1) * P], cur[:, 4 * q + k, :],
                                                   ident[:])
                    last.then_inc(s["t_done"], 1)

            stay_warm(banks[7], 14)
            transpose_tiles(lambda q: wait_normalised(pe, 0, q))
            pe.wait_ge(s["t_evac"], 4)
            pe.wait_ge(s["later_loaded"], W_LATER)
            for w, bank in ((wdl, banks[4]), (wb, banks[5])):
                for g in range(NG):
                    last = mm(bank[H * g:H * (g + 1), :], w[:], curT[:, g * GW:(g + 1) * GW],
                              start=True, stop=True)
                last.then_inc(s["scan_mm"], 1)
            for k in range(NT):
                mm(banks[k // 4][:, (k % 4) * P:(k % 4 + 1) * P], curT[:, k * P:(k + 1) * P], wd[:],
                   start=(k % 4 == 0), stop=False)
            stay_warm(banks[7], 14)
            pe.wait_ge(s["scan_h"], 1)
            for k in range(NT):
                g, c = k // GT, k % GT
                last = mm(banks[k // 4][:, (k % 4) * P:(k % 4 + 1) * P], sC[:, c * P:(c + 1) * P],
                          wc_own[:, g, :], start=False, stop=(k % 4 == 3))
                if k % 4 == 3:
                    last.then_inc(s["scan_out"], 1)

            stay_warm(banks[7], 24)
            pe.wait_ge(s["w1_loaded"], 16)
            pe.wait_ge(s["w2_loaded"], 16)
            pe.wait_ge(s["x2_ready"], 4)

            def one_layer(layer, parity, two):
                transpose_tiles(lambda q: pe.wait_ge(cur_loaded[q], (layer + 1) * 16))
                pe.wait_ge(s["t_evac"], layer * 4 + 8)
                pe.wait_ge(s["router_ready"], layer + 1)
                for g in range(4):
                    last = mm(banks[4][32 * g:32 * g + 32, :], rnow[:], curT[:, g * 512:(g + 1) * 512],
                              start=True, stop=True)
                last.then_inc(s["logits_done"], 1)
                pe.wait_ge(s["lgT_ready"], layer + 1)
                for c in range(4):
                    last = nc.tensor.transpose(banks[5][:, c * P:(c + 1) * P], lgT[:, c * P:(c + 1) * P],
                                               ident[:])
                last.then_inc(s["lg_done"], 1)
                stay_warm(banks[7], 10)
                pe.wait_ge(s["oh_ready"], layer + 1)
                def blocks(a, b):
                    return banks[6][:, a * E:b * E]

                for k in range(NT):
                    last = mm(blocks(k + 1, NT + 1).rearrange("p (k e) -> p k e", e=E), onesb[:],
                              ohb[:, k * E:(k + 1) * E].unsqueeze(1).broadcast_to([P, NT - k, E]),
                              start=(k == 0), stop=(k == NT - 1))
                    if k == 0:
                        mm(blocks(0, 1), trib[:], ohb[:, 0:E], start=False, stop=False)
                        mm(blocks(1, NT), trib[:], ohb[:, E:], start=False, stop=False)
                last.then_inc(s["rank_mm"], 1)
                stay_warm(banks[7], 16)
                pe.wait_ge(s["carried_ready"], layer + 1)
                for k in range(NT):
                    if k % (NT // 2) == 0:
                        pe.wait_ge(s["inv_in"], layer * 2 + (k // (NT // 2) + 1))
                    last = mm(banks[4][:, 0:NV * NT], ohr[:, k, :],
                              carried[:, k, :, :].rearrange("p v j -> p (v j)"),
                              start=(k == 0), stop=(k == NT - 1))
                last.then_inc(s["inv_done"], 1)
                stay_warm(banks[7], 10)
                wait_alone(pe, s["pieces_ready"], layer + 1)

                def count(j):
                    return layer * PIECES + j

                tile_of = [entry(piece_tile, 0, mybir.EngineType.PE, NT - 1)]

                def step(i):
                    if i < NT:
                        pe.wait_ge(gathered[i % 4], layer * OF_FOUR + (i // 4 + 1) * 16)
                        if i >= 2:
                            pe.wait_ge(s["xT_evac"], layer * NT + (i - 1))
                        nc.tensor.transpose(banks[i % 2][:, 0:P], xin[:, i % 4, :], ident[:]) \
                            .then_inc(s["xT_mm"], 1)
                    if 0 <= i - 1 < PIECES:
                        j = i - 1
                        if j < NT:
                            pe.wait_ge(s["xT_evac"], layer * NT + (j + 1))
                        pe.wait_ge(s["w1_staged"], count(j + 1))
                        if j >= 2:
                            pe.wait_ge(s["h_ready"], count(j - 1))
                        for c in range(FC):
                            last = mm(banks[2 + j % 2][:, c * P:(c + 1) * P],
                                      w1_piece[:, j % 2, c * P:(c + 1) * P], xT[:, ds(tile_of[j] * P, P)],
                                      start=True, stop=True)
                            if c == 1 and i < PIECES:
                                tile_of.append(entry(piece_tile, i, mybir.EngineType.PE, NT - 1))
                        last.then_inc(s["h_mm"], 1)
                    if 0 <= i - 2 < PIECES:
                        j = i - 2
                        e = entry(piece_expert, j, mybir.EngineType.PE, E - 1)
                        pe.wait_ge(s["h_ready"], count(j + 1))
                        if j >= 2:
                            pe.wait_ge(s["y_ready"], count(j - 1))
                        for c in range(FC):
                            last = mm(banks[6 + j % 2][:, 0:D], hh[:, j % 2, c * P:(c + 1) * P],
                                      w2[:, ds(e * FF + c * P, P)], start=(c == 0), stop=(c == FC - 1))
                        last.then_inc(s["y_mm"], 1)

                piece_steps(step)
                stay_warm(banks[5], 28)

            layers(pe, one_layer)

        @block.vector
        def _(dve):
            v = nc.vector
            step = [0]

            def link(ins):
                ins.then_inc(s["dve_step"], 1)
                step[0] += 1
                dve.wait_ge(s["dve_step"], step[0])

            def tile_stats(t):
                return v.bn_stats(st[:, ds(t, 1), :].rearrange("p a k -> p (a k)"),
                                  xs[:, ds(t, 1), :].rearrange("p a d -> p (a d)")).then_inc(s["x_stats"], 1)

            def finish_stats(n, done, tiles):
                dve.wait_ge(s["x_stats"], done)
                m, gap, r = mean[:, tiles], half_gap[:, tiles], rstd[:, tiles]
                v.tensor_tensor(m, st[:, tiles, 1], st[:, tiles, 4], ALU.add)
                v.tensor_tensor(gap, st[:, tiles, 1], st[:, tiles, 4], ALU.subtract)
                link(v.tensor_tensor(r, st[:, tiles, 2], st[:, tiles, 5], ALU.add))
                v.tensor_scalar(m, m, 0.5, None, ALU.mult)
                v.tensor_tensor(gap, gap, gap, ALU.mult)
                link(v.tensor_scalar(r, r, 1.0 / D, EPS, ALU.mult, ALU.add))
                v.scalar_tensor_tensor(r, gap, 0.25, r, ALU.mult, ALU.add).then_inc(s["stats_ready"], 1)

            def invert_std(n, tiles):
                dve.wait_ge(s["sqrt_ready"], n)
                link(v.reciprocal(rstd[:, tiles], rstd[:, tiles]))

            def normalise_even_quarters():
                v.scalar_tensor_tensor(offset[:], mean[:], -1.0, rstd[:], ALU.mult, ALU.mult) \
                    .then_inc(s["offset_ready"], 1)
                for q in (0, 2):
                    for t in range(4 * q, 4 * q + 4):
                        last = normalise(cur[:, t, :], t)
                    last.then_inc(s["ln_even"], 1)

            def normalise(out, t):
                return v.tensor_scalar(out, xs[:, ds(t, 1), :].rearrange("p a d -> p (a d)"),
                                       mean[:, ds(t, 1)],
                                       rstd[:, ds(t, 1)], ALU.subtract, ALU.mult)

            dve.wait_ge(s["x_first_loaded"], 16)
            for t in range(FIRST):
                tile_stats(t)
            finish_stats(1, FIRST, slice(0, FIRST))

            def make_masks():
                dve.wait_ge(s["w_loaded"], W_ATT)
                dve.wait_ge(s["consts_pool"], 4)
                v.tensor_scalar(mask_bias[0:S, :], mask_i[:], 0.0, MASKED, ALU.is_equal, ALU.mult)
                link(v.tensor_scalar(keep[:], mask_i[:], 0.0, None, ALU.not_equal))
                link(v.tensor_reduce(out=keep_any[:, 0:1], in_=keep[:], axis=AX, op=ALU.max))
                v.tensor_copy(keep_any[:, 1:P], keep_any[:, 0:1].broadcast_to([S, P - 1])) \
                    .then_inc(s["consts_dve"], 1)
                link(v.tensor_reduce(out=local[:], in_=head_of[:].rearrange("p (g j) -> p j g", j=4), axis=AX,
                                     op=ALU.add))
                link(v.tensor_copy(diag[:, 1, :, :], local[:].unsqueeze(2).broadcast_to([P, 4, S])))
                dve.wait_ge(s["consts_mm"], 1)
                v.tensor_tensor(diag[:, 0, :, :], banks[4][:, 0:S].unsqueeze(1).broadcast_to([P, 4, S]),
                                diag[:, 1, :, :], ALU.mult).then_inc(s["consts_dve"], 1)

            def xln_tile(t, u):
                if not isinstance(t, int) or t >= 2:
                    dve.wait_ge(s["tr_done"], t - 1)
                normalise(xln[:, u, :], t).then_inc(s["xln_ready"], 1)

            def values_evac(t, u):
                dve.wait_ge(s["proj_done"], t + 1)
                if not isinstance(t, int) or t >= 2:
                    dve.wait_ge(s["od_done"], 2 * (t - 1))
                v.tensor_tensor(vv[:, u, :].rearrange("p (b d) -> p b d", b=BT),
                                banks[7][:, 0:BT * D].rearrange("p (b d) -> p b d", b=BT),
                                bvr[:].unsqueeze(1).broadcast_to([P, BT, D]), ALU.add) \
                    .then_inc(s["v_evac"], 1)

            def scores_max(t, i, first):
                n = 4 * t + i
                dve.wait_ge(s["s_done"], n + 1)
                if not (first and i < 2):
                    dve.wait_ge(s["exp_done"], n - 1)
                v.tensor_reduce(out=nmax[:, i % 2, :], in_=banks[i % 2][:, :].rearrange("p (k t) -> p k t", k=4),
                                axis=AX, op=ALU.max, negate=True).then_inc(s["nmax_ready"], 1)

            def own_heads(t, u, b):
                m = 2 * t + b
                dve.wait_ge(s["od_done"], m + 1)
                if not isinstance(t, int) or m >= 1:
                    dve.wait_ge(s["od_summed"], m)
                v.tensor_tensor(od[:], banks[4][:, :], diag[:].rearrange("p w j s -> p (w j s)"), ALU.mult) \
                    .then_inc(s["od_read"], 1)
                dve.wait_ge(s["od_read"], m + 1)
                v.tensor_reduce(out=od_s[:, u, :, b, :], in_=od[:].rearrange("p (w j s) -> p w s j", w=2, j=4),
                                axis=AX, op=ALU.add).then_inc(s["od_summed"], 1)

            def attention_out(t, u):
                dve.wait_ge(s["od_summed"], 2 * t + 2)
                if not isinstance(t, int) or t >= 1:
                    dve.wait_ge(s["attn_ready"], t)
                v.reciprocal(rden[:], od_s[:, u, 1, :, :].rearrange("p b s -> p (b s)")) \
                    .then_inc(s["rden_ready"], 1)
                dve.wait_ge(s["rden_ready"], t + 1)
                v.tensor_tensor(attnT[:, u, :], od_s[:, u, 0, :, :].rearrange("p b s -> p (b s)"), rden[:],
                                ALU.mult).then_inc(s["attn_ready"], 1)

            def residual(t, u):
                xt = xs[:, ds(t, 1), :].rearrange("p a d -> p (a d)")
                v.tensor_tensor(xt, xt, bor[:], ALU.add).then_inc(s["xo_ready"], 1)
                dve.wait_ge(s["xo_ready"], t + 1)
                dve.wait_ge(s["wo_done"], t + 1)
                v.tensor_tensor(xt, banks[4][:, 0:D], xt, ALU.add).then_inc(s["x_updated"], 1)
                dve.wait_ge(s["x_updated"], t + 1)
                tile_stats(t)

            def tile(t, u, first, last):
                scores_max(t, 0, first)
                if not first:
                    own_heads(t - 1, 1 - u, 0)
                if not (isinstance(t, int) and t + 2 >= NT):
                    xln_tile(t + 2, u)
                scores_max(t, 1, first)
                if not first:
                    own_heads(t - 1, 1 - u, 1)
                scores_max(t, 2, first)
                if not first:
                    attention_out(t - 1, 1 - u)
                if not last:
                    values_evac(t + 1, 1 - u)
                scores_max(t, 3, first)
                if not first:
                    residual(t - 1, 1 - u)

            invert_std(1, slice(0, FIRST))
            xln_tile(0, 0)
            xln_tile(1, 1)
            make_masks()
            dve.wait_ge(s["x_loaded"], 16)
            for t in range(FIRST, NT):
                tile_stats(t)
            finish_stats(2, NT, slice(FIRST, NT))
            values_evac(0, 0)
            invert_std(2, slice(FIRST, NT))
            pairs_of_tiles(dve, tile, None, None)
            own_heads(NT - 1, 1, 0)
            own_heads(NT - 1, 1, 1)
            attention_out(NT - 1, 1)
            residual(NT - 1, 1)
            dve.wait_ge(s["later_loaded"], W_LATER)
            link(v.tensor_tensor(bcr[:], bcr[:], bdr[:], ALU.add))

            finish_stats(3, 2 * NT, slice(0, NT))
            invert_std(3, slice(0, NT))
            normalise_even_quarters()
            for q in (0, 2):
                dve.wait_ge(s["t_done"], q + 1)
                v.tensor_copy(curT[:, q * 512:(q + 1) * 512], banks[q][:, :]).then_inc(s["t_evac"], 1)
            dve.wait_ge(s["scan_abs"], 1)
            link(v.tensor_scalar(sA[:], banks[4][:, :], bdl4[:, 0:1], 0.0, ALU.add, ALU.max))
            link(v.tensor_scalar(a_tmp[:, 3:4], a4[:], 0.0, None, ALU.max))
            dve.wait_ge(s["scan_soft"], 1)
            link(v.tensor_tensor(a4[:], a_tmp[:, 2:3], a_tmp[:, 3:4], ALU.add))
            link(v.tensor_tensor(sA[:], sA[:], sC[:], ALU.add))
            link(v.tensor_scalar(sB[:], sA[:], a4[:, 0:1], -1.0, ALU.mult, ALU.mult))
            link(v.tensor_tensor_scan(sD[:], not_first[:], sB[:], 0.0, ALU.mult, ALU.add))
            v.tensor_scalar(sD[:], sD[:], -20.0, 20.0, ALU.max, ALU.min).then_inc(s["scan_cum"], 1)
            dve.wait_ge(s["scan_mm"], 2)
            v.scalar_tensor_tensor(sB[:], banks[5][:, :], bb4[:, 0:1], sA[:], ALU.add, ALU.mult) \
                .then_inc(s["scan_b"], 1)
            dve.wait_ge(s["scan_b"], 1)
            dve.wait_ge(s["scan_exp"], 1)
            link(v.tensor_tensor(sB[:].rearrange("p (b t) -> p b t", t=S),
                                 sB[:].rearrange("p (b t) -> p b t", t=S), decay[:, :, 0:S], ALU.mult))
            link(v.tensor_tensor_scan(sC[:], not_first[:], sB[:], 0.0, ALU.mult, ALU.add))
            dve.wait_ge(s["scan_exp"], 2)
            v.tensor_tensor(sC[:], sC[:], sA[:], ALU.mult).then_inc(s["scan_h"], 1)
            dve.wait_ge(s["xb_ready"], 1)
            for q in range(4):
                dve.wait_ge(s["scan_out"], q + 1)
                xq = xs[:, 4 * q:4 * q + 4, :].rearrange("p t d -> p (t d)")
                v.tensor_tensor(xq, banks[q][:, :], xq, ALU.add).then_inc(s["x2_ready"], 1)
                dve.wait_ge(s["x2_ready"], q + 1)
                for t in range(4 * q, 4 * q + 4):
                    tile_stats(t)
            finish_stats(4, 3 * NT, slice(0, NT))
            invert_std(4, slice(0, NT))
            normalise_even_quarters()

            base_steps = step[0]
            CHAIN = 33

            def one_layer(layer, parity, two):
                done = [0]

                def chain(ins):
                    ins.then_inc(s["dve_step"], 1)
                    done[0] += 1
                    dve.wait_ge(s["dve_step"], layer * CHAIN + (base_steps + done[0]))

                def ke(ap):
                    return ap.rearrange("p (k e) -> p k e", e=E)

                def over_e(ap):
                    return ap.unsqueeze(2).broadcast_to([P, NT, E])

                def over_k(ap):
                    return ap.unsqueeze(1).broadcast_to([P, NT, E])

                v.tensor_copy(rnow[:, 0:E], rt[:, ds(layer, 1), :].rearrange("p a e -> p (a e)")) \
                    .then_inc(s["router_ready"], 1)
                for q in (1, 3):
                    dve.wait_ge(s["t_done"], layer * 4 + (4 + q + 1))
                    v.tensor_copy(curT[:, q * 512:(q + 1) * 512], banks[q][:, :]).then_inc(s["t_evac"], 1)
                dve.wait_ge(s["logits_done"], layer + 1)
                v.tensor_copy(lgT[:], banks[4][:, :]).then_inc(s["lgT_ready"], 1)
                dve.wait_ge(s["lg_done"], layer + 1)
                logits = banks[5][:, :].rearrange("p (c j e) -> p j c e", c=4, j=4)[:, :, :, 0:E]

                def jc(ap):
                    return ap.rearrange("p (j c) -> p j c", j=4)

                chain(v.tensor_reduce(out=jc(mx[:]), in_=logits, axis=AX, op=ALU.max))
                v.tensor_tensor(ex[:].rearrange("p (j c e) -> p j c e", j=4, c=4), logits,
                                jc(mx[:]).unsqueeze(3).broadcast_to([P, 4, 4, E]), ALU.subtract) \
                    .then_inc(s["sh_ready"], 1)
                dve.wait_ge(s["ex_ready"], layer + 1)
                chain(v.tensor_reduce(out=mx[:], in_=ke(ex[:]), axis=AX, op=ALU.max))
                chain(v.tensor_tensor(ke(eq[:]), ke(ex[:]), over_e(mx[:]), ALU.is_equal))
                chain(v.tensor_tensor_scan(nth[:], not_first16[:], eq[:], 0.0, ALU.mult, ALU.add))
                v.scalar_tensor_tensor(ohb[:], nth[:], 1.0, eq[:], ALU.is_equal, ALU.mult) \
                    .then_inc(s["oh_ready"], 1)
                chain(v.tensor_reduce(out=sm[:], in_=ke(ex[:]), axis=AX, op=ALU.add))
                chain(v.reciprocal(sm[:], sm[:]))
                chain(v.tensor_tensor(wt[:], mx[:], sm[:], ALU.mult))
                chain(v.tensor_copy(vals[:, :, 2], wt[:]))
                chain(v.tensor_tensor(wr[:], wt[:], vals[:, :, 2], ALU.subtract))
                chain(v.tensor_copy(vals[:, :, 3], wr[:]))
                v.tensor_tensor(vals[:, :, 4], wr[:], vals[:, :, 3], ALU.subtract)
                dve.wait_ge(s["rank_mm"], layer + 1)
                counts = banks[6][:, NT * E:(NT + 1) * E]
                chain(v.tensor_tensor_scan(ends[:], ones[:, 0:E], counts, 0.0, ALU.mult, ALU.add))
                chain(v.tensor_tensor(starts[:], ends[:], counts, ALU.subtract))
                chain(v.tensor_tensor(ke(rk[:]), ke(banks[6][:, 0:NT * E]), over_k(starts[:]), ALU.add))
                chain(v.tensor_tensor(rk[:], rk[:], ohb[:], ALU.mult))
                chain(v.tensor_reduce(out=place[:], in_=ke(rk[:]), axis=AX, op=ALU.add))
                chain(v.tensor_copy(place_i[:], place[:]))
                v.tensor_scalar(row_i[:], place_i[:], P - 1, None, ALU.bitwise_and)
                chain(v.tensor_scalar(tile_i[:], place_i[:], P.bit_length() - 1, None, ALU.logical_shift_right))
                v.tensor_tensor(oht[:], iota_r[:, 0:NT].unsqueeze(1).broadcast_to([P, NT, NT]),
                                tile_i[:].unsqueeze(2).broadcast_to([P, NT, NT]), ALU.is_equal) \
                    .then_inc(s["tiles_hot"], 1)
                dve.wait_ge(s["tiles_hot"], layer + 1)
                for n in range(2):
                    v.tensor_tensor(carried[:, :, n, :], oht[:],
                                    vals[:, :, n:n + 1].broadcast_to([P, NT, NT]), ALU.mult)
                for half in range(2):
                    a = slice(half * NT // 2, (half + 1) * NT // 2)
                    v.tensor_tensor(ohr[:, a, :], iota_r[:].unsqueeze(1).broadcast_to([P, NT // 2, P]),
                                    row_i[:, a].unsqueeze(2).broadcast_to([P, NT // 2, P]), ALU.is_equal) \
                        .then_inc(s["inv_in"], 1)
                chain(v.tensor_tensor(ends_cmp[:], over_e(sorted_pos[:]), over_k(ends[:]), ALU.is_ge))
                chain(v.tensor_reduce(out=expert_at[:], in_=ends_cmp[:], axis=AX, op=ALU.add))
                dve.wait_ge(s["inv_done"], layer + 1)
                inv = banks[4][:, 0:NV * NT].rearrange("p (v j) -> p v j", v=NV)
                chain(v.tensor_copy(token[:], inv[:, 0, :]))
                v.tensor_tensor(token_i[:], inv[:, 1, :], token[:], ALU.add).then_inc(s["tokens_ready"], 1)
                chain(v.tensor_copy(end_i[:], ends[0:1, :]))
                chain(v.tensor_scalar(end_i[:], end_i[:], P.bit_length() - 1, None, ALU.logical_shift_right))
                chain(v.tensor_tensor(first_piece[:], end_i[:], iota_e1[:], ALU.add))
                chain(v.tensor_tensor(pcmp[:], iota_j[0:1, :].unsqueeze(2).broadcast_to([1, PC, E - 1]),
                                      first_piece[:, 0:E - 1].unsqueeze(1).broadcast_to([1, PC, E - 1]),
                                      ALU.is_ge))
                chain(v.tensor_reduce(out=pexp[:], in_=pcmp[:], axis=AX, op=ALU.add))
                v.tensor_copy(piece_expert[:], pexp[:])
                chain(v.tensor_tensor(pexp_tile[:], iota_j[0:1, :], pexp[:], ALU.subtract))
                v.tensor_scalar(piece_tile[:], pexp_tile[:], float(NT - 1), None, ALU.min) \
                    .then_inc(s["pieces_ready"], 1)
                chain(v.tensor_tensor(piece_at[:], expert_at[:], iota_r[:, 0:NT], ALU.add))
                chain(v.tensor_tensor(piece_hot[:], iota_j[:].unsqueeze(2).broadcast_to([P, PC, NT]),
                                      piece_at[:].unsqueeze(1).broadcast_to([P, PC, NT]), ALU.is_equal))
                chain(v.tensor_copy(wsort[:], inv[:, 2, :]))
                chain(v.tensor_tensor(wsort[:], inv[:, 3, :], wsort[:], ALU.add))
                chain(v.tensor_tensor(wsort[:], inv[:, 4, :], wsort[:], ALU.add))
                chain(v.scalar_tensor_tensor(piece_hot[:], piece_hot[:], 0.5,
                                             wsort[:].unsqueeze(1).broadcast_to([P, PC, NT]),
                                             ALU.mult, ALU.mult))
                chain(v.tensor_reduce(out=wpiece[:], in_=piece_hot[:], axis=AX, op=ALU.add))
                assert done[0] == CHAIN, done
                dve.wait_ge(s["pieces_ready"], layer + 1)
                dve.wait_ge(s["y_zeroed"], layer + 1)

                def count(j):
                    return layer * PIECES + j

                def step(i):
                    if 0 <= i - 1 < PIECES:
                        j = i - 1
                        dve.wait_ge(s["tanh_done"], count(j + 1))
                        if j >= 2:
                            dve.wait_ge(s["y_mm"], count(j - 1))
                        v.scalar_tensor_tensor(hh[:, j % 2, :], th[:, j % 2, :], 1.0, banks[2 + j % 2][:, :],
                                               ALU.add, ALU.mult).then_inc(s["h_ready"], 1)
                    if 0 <= i - 2 < PIECES:
                        j = i - 2
                        tile_of = entry(piece_tile, j, mybir.EngineType.DVE, NT - 1)
                        dve.wait_ge(s["y_mm"], count(j + 1))
                        if j >= 1:
                            dve.wait_ge(s["y_ready"], count(j))
                        sorted_tile = ysort[:, ds(tile_of, 1), :].rearrange("p a d -> p (a d)")
                        v.scalar_tensor_tensor(sorted_tile, banks[6 + j % 2][:, 0:D], wpiece[:, j:j + 1],
                                               sorted_tile, ALU.mult, ALU.add).then_inc(s["y_ready"], 1)

                piece_steps(step)

            layers(dve, one_layer)
            for q in range(4):
                dve.wait_ge(cur_loaded[q], (L + 1) * 16)
                xq = xs[:, 4 * q:4 * q + 4, :]
                v.tensor_tensor(xq, xq, cur[:, 4 * q:4 * q + 4, :], ALU.add).then_inc(s["out_ready"], 1)


_INS = ['x', 'ctx_1024', 'mask_SxS2_ik0', 'L0_xattn_Wq', 'L0_xattn_bq', 'L0_xattn_Wk', 'L0_xattn_bk',
        'L0_xattn_Wv', 'L0_xattn_bv', 'L0_xattn_Wo', 'L0_xattn_bo', 'L0_attn_A', 'L0_attn_Wb',
        'L0_attn_bb', 'L0_attn_Wc', 'L0_attn_bc', 'L0_attn_Wd', 'L0_attn_bd', 'L0_attn_Wdelta',
        'L0_attn_bdelta', 'L0_ffn_routers', 'L0_ffn_W1', 'L0_ffn_W2']


def kernel(**inputs):
    import numpy as _np
    import concourse.bacc as _bacc
    from concourse import mybir as _mybir
    from concourse.bass_utils import run_bass_kernel_spmd as _run

    nc = _bacc.Bacc("TRN2", target_bir_lowering=False, num_devices=1)
    arrays, args = {}, []
    for name in _INS:
        a = _np.ascontiguousarray(inputs[name])
        arrays[f"in_{name}_dram"] = a
        args.append(nc.dram_tensor(f"in_{name}_dram", a.shape, _mybir.dt.from_np(a.dtype), kind="ExternalInput").ap())
    shape = inputs["x"].shape
    args.append(nc.dram_tensor("out_0_dram", shape, _mybir.dt.from_np(_np.dtype("float32")), kind="ExternalOutput").ap())
    perceiver_block(nc, *args)
    r = _run(nc, [arrays], core_ids=[0])
    return r.results[0]["out_0_dram"]
```
